# Optimizing a Trainium2 kernel written in Bass

```python
import numpy as np
import jax
import jax.numpy as jnp

def _softmax(x, axis=-1):
    return jax.nn.softmax(x, axis=axis)

def _gelu(x):
    return jax.nn.gelu(x, approximate=True)

def _silu(x):
    return jax.nn.silu(x)

def _sigmoid(x):
    return jax.nn.sigmoid(x)

def _layernorm(x, axis=-1, eps=1e-05):
    m = jnp.mean(x, axis=axis, keepdims=True)
    v = jnp.var(x, axis=axis, keepdims=True)
    return (x - m) / jnp.sqrt(v + eps)

def _scatter_add(tgt, idx, src, axis=0):
    return tgt.at[idx].add(src)

def _segment_sum(src, seg, n):
    return jax.ops.segment_sum(src, seg, n)
kernel_name = 'mk_prb_d2_jaxref_r8_26be14'

def setup_inputs(seed: int=0):
    np.random.seed(seed)
    _w = jnp.asarray

    def _L0_attn_setup():
        import jax, jax.numpy as jnp
        import numpy as np
        EMBED_DIM = 128
        NUM_HEADS = 16
        BATCH = 4
        SEQ = 512
        key = jax.random.key(seed)
        ks = jax.random.split(key, 5)
        scale = 0.02
        E = EMBED_DIM
        x = jax.random.normal(ks[0], (BATCH, SEQ, E), dtype=jnp.float32)
        Wq = jax.random.normal(ks[1], (E, E), dtype=jnp.float32) * scale
        Wk = jax.random.normal(ks[2], (E, E), dtype=jnp.float32) * scale
        Wv = jax.random.normal(ks[3], (E, E), dtype=jnp.float32) * scale
        Wo = jax.random.normal(ks[4], (E, E), dtype=jnp.float32) * scale
        z = jnp.zeros((E,), dtype=jnp.float32)
        return {'x': x, 'Wq': Wq, 'bq': z, 'Wk': Wk, 'bk': z, 'Wv': Wv, 'bv': z, 'Wo': Wo, 'bo': z}
    _L0_attn_in = _L0_attn_setup()

    def _L0_ffn_setup():
        import jax, jax.numpy as jnp
        import numpy as np
        HIDDEN = 128
        N_EXPERTS = 8
        TOP_K = 2
        INTER = 176
        N_SHARED = 2
        SCALE = 1.0
        key = jax.random.key(seed)
        ks = jax.random.split(key, 9)
        s_h = 1.0 / np.sqrt(HIDDEN)
        s_i = 1.0 / np.sqrt(INTER)
        x = jax.random.normal(ks[0], (2, 256, HIDDEN), dtype=jnp.float32)
        gate_w = jax.random.uniform(ks[1], (N_EXPERTS, HIDDEN), jnp.float32, -s_h, s_h)
        wg = jax.random.uniform(ks[2], (N_EXPERTS, HIDDEN, INTER), jnp.float32, -s_h, s_h)
        wu = jax.random.uniform(ks[3], (N_EXPERTS, HIDDEN, INTER), jnp.float32, -s_h, s_h)
        wd = jax.random.uniform(ks[4], (N_EXPERTS, INTER, HIDDEN), jnp.float32, -s_i, s_i)
        si = INTER * N_SHARED
        s_si = 1.0 / np.sqrt(si)
        swg = jax.random.uniform(ks[5], (HIDDEN, si), jnp.float32, -s_h, s_h)
        swu = jax.random.uniform(ks[6], (HIDDEN, si), jnp.float32, -s_h, s_h)
        swd = jax.random.uniform(ks[7], (si, HIDDEN), jnp.float32, -s_si, s_si)
        return {'x': x, 'gate_w': gate_w, 'wg': wg, 'wu': wu, 'wd': wd, 'swg': swg, 'swu': swu, 'swd': swd}
    _L0_ffn_in = _L0_ffn_setup()

    def _L1_attn_setup():
        import jax, jax.numpy as jnp
        import numpy as np
        B, N, E, H = (2, 256, 128, 8)
        HID = 128
        D = HID // H
        EPS = 1e-08

        def rms_norm(x, scale):
            rms = jnp.linalg.norm(x, axis=-1, keepdims=True) * x.shape[-1] ** (-0.5)
            return scale * (x / (rms + EPS))
        key = jax.random.key(seed)
        ks = jax.random.split(key, 12)
        s = 0.02
        return {'x': jax.random.normal(ks[0], (B, N, E), jnp.float32), 'Wq': jax.random.normal(ks[1], (HID, E), jnp.float32) * s, 'bq': jnp.zeros((HID,), jnp.float32), 'Wk': jax.random.normal(ks[2], (HID, E), jnp.float32) * s, 'bk': jnp.zeros((HID,), jnp.float32), 'Wv': jax.random.normal(ks[3], (HID, E), jnp.float32) * s, 'bv': jnp.zeros((HID,), jnp.float32), 'Wu': jax.random.normal(ks[4], (HID, E), jnp.float32) * s, 'bu': jnp.zeros((HID,), jnp.float32), 'Wo': jax.random.normal(ks[5], (E, HID), jnp.float32) * s, 'bo': jnp.zeros((E,), jnp.float32), 'scale': jnp.ones((HID,), jnp.float32)}
    _L1_attn_in = _L1_attn_setup()

    def _L1_ffn_setup():
        import jax, jax.numpy as jnp
        import numpy as np
        TOP_K = 2
        key = jax.random.key(seed)
        ks = jax.random.split(key, 5)
        B, T, C, D, E = (2, 256, 128, 512, 8)
        init = 0.02
        return {'x': jax.random.normal(ks[0], (B, T, C), dtype=jnp.float32), 'w_router': jax.random.normal(ks[1], (E, C), dtype=jnp.float32) * init, 'w1': jax.random.normal(ks[2], (E, C, D), dtype=jnp.float32) * init, 'b1': jnp.zeros((E, D), dtype=jnp.float32), 'w2': jax.random.normal(ks[3], (E, D, C), dtype=jnp.float32) * init, 'b2': jnp.zeros((E, C), dtype=jnp.float32)}
    _L1_ffn_in = _L1_ffn_setup()
    _d = {'L0_attn_x': _L0_attn_in['x'], 'L0_attn_Wq': _L0_attn_in['Wq'], 'L0_attn_bq': _L0_attn_in['bq'], 'L0_attn_Wk': _L0_attn_in['Wk'], 'L0_attn_bk': _L0_attn_in['bk'], 'L0_attn_Wv': _L0_attn_in['Wv'], 'L0_attn_bv': _L0_attn_in['bv'], 'L0_attn_Wo': _L0_attn_in['Wo'], 'L0_attn_bo': _L0_attn_in['bo'], 'L0_ffn_gate_w': _L0_ffn_in['gate_w'], 'L0_ffn_wg': _L0_ffn_in['wg'], 'L0_ffn_wu': _L0_ffn_in['wu'], 'L0_ffn_wd': _L0_ffn_in['wd'], 'L0_ffn_swg': _L0_ffn_in['swg'], 'L0_ffn_swu': _L0_ffn_in['swu'], 'L0_ffn_swd': _L0_ffn_in['swd'], 'L1_attn_Wq': _L1_attn_in['Wq'], 'L1_attn_bq': _L1_attn_in['bq'], 'L1_attn_Wk': _L1_attn_in['Wk'], 'L1_attn_bk': _L1_attn_in['bk'], 'L1_attn_Wv': _L1_attn_in['Wv'], 'L1_attn_bv': _L1_attn_in['bv'], 'L1_attn_Wu': _L1_attn_in['Wu'], 'L1_attn_bu': _L1_attn_in['bu'], 'L1_attn_Wo': _L1_attn_in['Wo'], 'L1_attn_bo': _L1_attn_in['bo'], 'L1_attn_scale': _L1_attn_in['scale'], 'L1_ffn_w_router': _L1_ffn_in['w_router'], 'L1_ffn_w1': _L1_ffn_in['w1'], 'L1_ffn_b1': _L1_ffn_in['b1'], 'L1_ffn_w2': _L1_ffn_in['w2'], 'L1_ffn_b2': _L1_ffn_in['b2']}
    _x0 = _d['L0_attn_x']
    _d['L0_attn_x'] = jax.random.normal(jax.random.fold_in(jax.random.key(seed), 1), (32, 256, 128), dtype=_x0.dtype)
    del _x0
    return _d

def reference(L0_attn_x, L0_attn_Wq, L0_attn_bq, L0_attn_Wk, L0_attn_bk, L0_attn_Wv, L0_attn_bv, L0_attn_Wo, L0_attn_bo, L0_ffn_gate_w, L0_ffn_wg, L0_ffn_wu, L0_ffn_wd, L0_ffn_swg, L0_ffn_swu, L0_ffn_swd, L1_attn_Wq, L1_attn_bq, L1_attn_Wk, L1_attn_bk, L1_attn_Wv, L1_attn_bv, L1_attn_Wu, L1_attn_bu, L1_attn_Wo, L1_attn_bo, L1_attn_scale, L1_ffn_w_router, L1_ffn_w1, L1_ffn_b1, L1_ffn_w2, L1_ffn_b2):

    def _L0_attn_ref(x, Wq, bq, Wk, bk, Wv, bv, Wo, bo):
        import jax, jax.numpy as jnp
        import numpy as np
        EMBED_DIM = 128
        NUM_HEADS = 16
        BATCH = 4
        SEQ = 512
        B, S, E = x.shape
        H = NUM_HEADS
        D = E // H

        def proj(W, b):
            return (jnp.einsum('bse,fe->bsf', x, W) + b).reshape(B, S, H, D)
        q = jax.nn.elu(proj(Wq, bq)) + 1.0
        k = jax.nn.elu(proj(Wk, bk)) + 1.0
        v = proj(Wv, bv)
        kv = jnp.einsum('bshd,bshe->bhde', k, v)
        out = jnp.einsum('bshd,bhde->bshe', q, kv).reshape(B, S, E)
        out = jnp.einsum('bse,fe->bsf', out, Wo) + bo
        return out

    def _L0_ffn_ref(x, gate_w, wg, wu, wd, swg, swu, swd):
        import jax, jax.numpy as jnp
        import numpy as np
        HIDDEN = 128
        N_EXPERTS = 8
        TOP_K = 2
        INTER = 176
        N_SHARED = 2
        SCALE = 1.0
        B, S, H = x.shape
        xf = x.reshape(-1, H)
        T = xf.shape[0]
        logits = xf.astype(jnp.float32) @ gate_w.astype(jnp.float32).T
        scores = jax.nn.softmax(logits, axis=-1)
        topw, topi = jax.lax.top_k(scores, TOP_K)
        denom = topw.sum(axis=-1, keepdims=True) + 1e-20
        topw = topw / denom * SCALE
        wdense = jnp.zeros((T, N_EXPERTS), jnp.float32).at[jnp.arange(T)[:, None], topi].set(topw)
        hg = jnp.einsum('th,ehi->eti', xf, wg)
        hu = jnp.einsum('th,ehi->eti', xf, wu)
        eo = jnp.einsum('eti,eih->eth', jax.nn.silu(hg) * hu, wd)
        y = jnp.einsum('te,eth->th', wdense, eo)
        shared = jax.nn.silu(xf @ swg) * (xf @ swu) @ swd
        return (y + shared).reshape(B, S, H)

    def _L1_attn_ref(x, Wq, bq, Wk, bk, Wv, bv, Wu, bu, Wo, bo, scale):
        import jax, jax.numpy as jnp
        import numpy as np
        B, N, E, H = (2, 256, 128, 8)
        HID = 128
        D = HID // H
        EPS = 1e-08

        def rms_norm(x, scale):
            rms = jnp.linalg.norm(x, axis=-1, keepdims=True) * x.shape[-1] ** (-0.5)
            return scale * (x / (rms + EPS))
        n = x.shape[-2]
        q = x @ Wq.T + bq
        u = x @ Wu.T + bu
        k = x @ Wk.T + bk
        v = x @ Wv.T + bv
        u = jax.nn.silu(u)
        v = jax.nn.silu(v)
        to_heads = lambda t: t.reshape(*t.shape[:-1], H, D).swapaxes(-3, -2)
        q, k, v = map(to_heads, (q, k, v))
        q = jax.nn.elu(q)
        k = jax.nn.elu(k)
        mask = jnp.tril(jnp.ones((n, n), q.dtype))
        energy = jnp.einsum('bhnd,bhmd->bhnm', q, k) * mask
        out = jnp.einsum('bhnm,bhmd->bhnd', energy, v)
        out = out.swapaxes(-3, -2).reshape(*x.shape[:-1], HID)
        out = rms_norm(out, scale)
        out = u * out
        return out @ Wo.T + bo

    def _L1_ffn_ref(x, w_router, w1, b1, w2, b2):
        import jax, jax.numpy as jnp
        import numpy as np
        TOP_K = 2
        B, T, C = x.shape
        E = w_router.shape[0]
        xf = x.reshape(B * T, C)
        N = xf.shape[0]
        logits = jnp.einsum('nc,ec->ne', xf, w_router)
        probs = jax.nn.softmax(logits, axis=-1)
        topw, topi = jax.lax.top_k(probs, TOP_K)
        topw = topw / jnp.sum(topw, axis=-1, keepdims=True)
        wdense = jnp.zeros((N, E), dtype=xf.dtype)
        wdense = wdense.at[jnp.arange(N)[:, None], topi].set(topw)
        h = jax.nn.gelu(jnp.einsum('nc,ecd->ned', xf, w1) + b1[None, :, :], approximate=False)
        expert_out = jnp.einsum('ned,edc->nec', h, w2) + b2[None, :, :]
        out = jnp.einsum('ne,nec->nc', wdense, expert_out)
        return out.reshape(B, T, C)
    x = L0_attn_x
    xn = _layernorm(x, axis=-1)
    x = x + _L0_attn_ref(xn, L0_attn_Wq, L0_attn_bq, L0_attn_Wk, L0_attn_bk, L0_attn_Wv, L0_attn_bv, L0_attn_Wo, L0_attn_bo) + _L0_ffn_ref(xn, L0_ffn_gate_w, L0_ffn_wg, L0_ffn_wu, L0_ffn_wd, L0_ffn_swg, L0_ffn_swu, L0_ffn_swd)
    xn = _layernorm(x, axis=-1)
    x = x + _L1_attn_ref(xn, L1_attn_Wq, L1_attn_bq, L1_attn_Wk, L1_attn_bk, L1_attn_Wv, L1_attn_bv, L1_attn_Wu, L1_attn_bu, L1_attn_Wo, L1_attn_bo, L1_attn_scale) + _L1_ffn_ref(xn, L1_ffn_w_router, L1_ffn_w1, L1_ffn_b1, L1_ffn_w2, L1_ffn_b2)
    return x

_drawn_inputs = setup_inputs


def setup_inputs(seed=0):
    import zlib

    import numpy as np

    out = dict(_drawn_inputs(seed))
    spreads = {'L0_attn_bq': (0.0, 0.457),
     'L0_attn_bk': (0.0, 0.286),
     'L0_attn_bv': (0.0, 0.1),
     'L0_attn_bo': (0.0, 2.0),
     'L1_attn_bq': (0.0, 2.0),
     'L1_attn_bk': (0.0, 2.0),
     'L1_attn_bv': (0.0, 2.0),
     'L1_attn_bu': (0.0, 2.0),
     'L1_attn_bo': (0.0, 2.0),
     'L1_attn_scale': (1.0, 0.6),
     'L1_ffn_b1': (0.0, 2.0),
     'L1_ffn_b2': (0.0, 2.0)}
    factors = {'L0_attn_Wk': 2.681,
     'L0_ffn_gate_w': 8.0,
     'L0_ffn_wg': 8.0,
     'L0_ffn_wu': 8.0,
     'L0_ffn_wd': 8.0,
     'L0_ffn_swg': 8.0,
     'L0_ffn_swu': 8.0,
     'L0_ffn_swd': 8.0,
     'L1_attn_Wq': 21.827,
     'L1_attn_Wk': 31.052,
     'L1_attn_Wv': 23.415,
     'L1_attn_Wu': 8.0,
     'L1_attn_Wo': 8.0,
     'L1_ffn_w_router': 8.0,
     'L1_ffn_w1': 8.0,
     'L1_ffn_w2': 8.0}
    for name, (base, spread) in spreads.items():
        noise = np.random.default_rng([zlib.crc32(name.encode()), seed]).standard_normal(out[name].shape)
        drawn = base * np.exp(spread * noise) if base else spread * noise
        out[name] = jnp.asarray(drawn.astype(out[name].dtype))
    for name, factor in factors.items():
        out[name] = (out[name] * factor).astype(out[name].dtype)
    return out
```

```python
from collections import deque
from contextlib import ExitStack

import concourse.bass as bass
import numpy as np
from concourse import mybir
from concourse.alu_op_type import AluOpType as ALU

F32 = mybir.dt.float32
I32 = mybir.dt.int32
BF16 = mybir.dt.bfloat16
ACT = mybir.ActivationFunctionType
AX = mybir.AxisListType.X

P = 128
B, S, C = 32, 256, 128
TOK = B * S
NT = TOK // P
GT = 4
NG = NT // GT
ST = 16
NS = NT // ST
E = 8
K = 2
SLOTS = 512
SUB = SLOTS // P
NTILES = (K * TOK - E) // SLOTS + E
REGION = TOK + SLOTS
DUMMY = E * REGION
NDUMMY = NTILES - K * TOK // SLOTS
ROW = C + 2
TRASH = K * TOK
NPAD = E + NDUMMY
H0, D0 = 16, 8
H1, D1 = 8, 16
HEADS32 = 32 // D1
F0 = 176
F0P = 192
F0T = F0 - P
FS = 352
FSC = [(0, 128), (128, 128), (256, 96)]
F1 = 512
NC1 = F1 // P
W0COLS = 2 * F0P + 2 * C
W1COLS = F1 + NC1 * C + NC1 + C
LN_EPS = 1e-5
RMS_EPS = 1e-8
GATE_EPS = 1e-20
BIG = 3.0e38


def constants():
    p = np.arange(P)
    blocks = {
        "ident": np.eye(P),
        "before": p[:, None] < p[None, :],
        "causal": 0.5 * (p[:, None] <= p[None, :]),
        "heads0": p[:, None] // D0 == p[None, :] // D0,
        "heads1": 0.5 * (p[:, None] // D1 == p[None, :] // D1),
        "parity": (p[:, None] // D1) % HEADS32 == np.arange(HEADS32)[None, :],
        "first": np.broadcast_to(E - np.arange(E), (P, E)),
        "regions": np.broadcast_to(np.arange(E) * REGION, (P, E)),
        "tiles": np.broadcast_to(np.arange(NTILES), (P, NTILES)),
    }
    at, cols = {}, 0
    for name, block in blocks.items():
        at[name] = (cols, block.shape[1])
        cols += block.shape[1]
    return np.concatenate([b.astype(np.float32) for b in blocks.values()], axis=1), at


def return_addresses():
    token = np.arange(NT)[None, :] * P + np.arange(P)[:, None]
    return np.stack([token + k * TOK for k in range(K)], axis=1).astype(np.int32)


def padding_addresses():
    n = np.arange(NPAD * SUB).reshape(1, NPAD, SUB)
    return (TRASH + n * P + np.arange(P).reshape(P, 1, 1)).astype(np.int32)


class Line:

    def __init__(self, engine, sem):
        self.e, self.sem, self.n, self.met = engine, sem, 0, {}

    def need(self, *marks):
        for sem, n in marks:
            if self.met.get(sem.name, 0) < n:
                self.e.wait_ge(sem, n)
                self.met[sem.name] = n

    def did(self, ins):
        self.n += 1
        ins.then_inc(self.sem, 1)
        return (self.sem, self.n)


class Arrival:

    def __init__(self, sem):
        self.sem, self.n = sem, 0

    def by(self, ins):
        self.n += 16
        ins.then_inc(self.sem, 16)
        return (self.sem, self.n)

    @property
    def all(self):
        return (self.sem, self.n)


class Slot:

    def __init__(self, ap, arrival=None):
        self.ap, self.freed, self.arrival = ap, (), arrival


class Ring:
    def __init__(self, slots):
        self.free = deque(slots)

    def take(self):
        return self.free.popleft()

    def give(self, slot, *marks):
        slot.freed = marks
        self.free.append(slot)


def in_turn(works, depth):
    works, active = iter(works), []
    while True:
        if len(active) < depth:
            nxt = next(works, None)
            if nxt is not None:
                active.append(nxt)
        if not active:
            return
        active = [w for w in active if next(w, "done") != "done"]


def build(nc, t, out):
    const_np, at = constants()
    with ExitStack() as ctx:
        def sb(name, shape, dt=F32):
            return ctx.enter_context(nc.sbuf_tensor(name, shape, dt))

        def sem(name):
            return ctx.enter_context(nc.semaphore(name))

        pe = Line(nc.tensor, sem("pe_done"))
        dve = Line(nc.vector, sem("dve_done"))
        act = Line(nc.scalar, sem("act_done"))
        pool = Line(nc.gpsimd, sem("pool_done"))
        sp = Line(nc.sync, sem("sp_done"))
        sp_e, act_e, dve_e, pe_e, pool_e = sp.e, act.e, dve.e, pe.e, pool.e

        sent = nc.dram_tensor("sent", (DUMMY + NDUMMY * SLOTS, ROW), F32, kind="Internal").ap()
        back = nc.dram_tensor("back", (TRASH + NPAD * SLOTS, C), F32, kind="Internal").ap()

        X = sb("X", [P, NT, C])
        xT = sb("xT", [P, NT, P])
        consts = sb("consts", [P, const_np.shape[1]])
        addresses = sb("addresses", [P, K, NT], I32)
        w_attn0 = sb("w_attn0", [P, 4 * C])
        w_attn1 = sb("w_attn1", [P, 5 * C])
        w_shared = sb("w_shared", [P, 2 * FS + 3 * C])
        gates = sb("gates", [P, 2 * E])
        cols = sb("cols", [P, 5])
        brow = sb("brow", [1, 2 * C + C + 2 * C])
        bo1 = sb("bo1", [P, C])
        ones = sb("ones", [1, P])
        ones_bf = sb("ones_bf", [P, P], BF16)
        before_bf = sb("before_bf", [P, P], BF16)
        bq0p1 = sb("bq0p1", [P, 1])
        wo1s = sb("wo1s", [P, C])
        pad_addresses = sb("pad_addresses", [P, NPAD, SUB], I32)
        pads = sb("pads", [P, E, SUB, ROW])

        def const(name):
            a, n = at[name]
            return consts[:, a:a + n]

        ident = const("ident")
        banks = [Slot(ctx.enter_context(nc.psum_tensor(f"bank{i}", [P, 512], F32))) for i in range(8)]
        psum = Ring(banks)

        def ring(name, n, shape, dt=F32, dma=False):
            return Ring([Slot(sb(f"{name}{i}", shape, dt), Arrival(sem(f"{name}{i}_dma")) if dma else None)
                         for i in range(n)])

        rows_ring = ring("rows", 2, [P, ST, K, ROW], dma=True)
        big = ring("big", 9, [P, 512])
        small = ring("small", 6, [P, P])

        x_in = t["x"].rearrange("(n p) c -> p n c", p=P)
        x_arrival = [Arrival(sem(f"x{s}_dma")) for s in range(NS)]
        const_arrival = Arrival(sem("const_dma"))
        weight_arrival = Arrival(sem("weight_dma"))
        x_here = []

        def load_x(s):
            a = x_arrival[s]
            for h in range(2):
                j = ST * s + 8 * h
                a.by(sp_e.dma_start(X[:, j:j + 8, :], x_in[:, j:j + 8, :]))
            x_here.append(a.all)

        load_x(0)
        for dst, src in ((consts[:], t["consts"]), (addresses[:], t["addresses"]), (pad_addresses[:], t["pad_addresses"]), (gates[:], t["gates"]),
                         (cols[:], t["cols"]), (brow[:], t["brow"])):
            const_arrival.by(act_e.dma_start(dst, src))
        consts_here = const_arrival.all
        for dst, src in ((w_attn0[:], t["w_attn0"]), (w_attn1[:], t["w_attn1"]),
                         (w_shared[:], t["w_shared"]), (bo1[:], t["bo1"])):
            weight_arrival.by(act_e.dma_start(dst, src))
        weights_here = weight_arrival.all
        for s in range(1, NS):
            load_x(s)

        dve.did(dve_e.memset(ones[:], 1.0))
        dve.did(dve_e.memset(ones_bf[:], 1.0))
        zeroed = dve.did(dve_e.memset(pads[:], 0.0))
        dve.need(consts_here)
        dve.did(dve_e.tensor_copy(before_bf[:], const("before")))
        dve.did(dve_e.tensor_scalar(bq0p1[:], cols[:, 0:1], 1.0, None, ALU.add))
        dve.need(zeroed)
        dummies = dve.did(dve_e.tensor_copy(pads[:, 0:NDUMMY, :, C].bitcast(I32), pad_addresses[:, E:NPAD, :]))
        dve.need(weights_here)
        made = dve.did(dve_e.tensor_scalar(wo1s[:], w_attn1[:, 4 * C:5 * C], cols[:, 3:4], 0.5, ALU.mult, ALU.mult))
        pe.need(consts_here, weights_here, made)
        act.need(consts_here, weights_here, made)
        pad_arrival = Arrival(sem("pad_dma"))
        sp.need(dummies)
        for d in range(NDUMMY):
            first = DUMMY + d * SLOTS
            pad_arrival.by(sp_e.dma_start(sent[first:first + SLOTS, :].rearrange("(s p) c -> p s c", p=P), pads[:, d, :, :]))
        dve.need(pad_arrival.all)
        pads_ready = dve.did(dve_e.tensor_copy(pads[:, :, :, C].bitcast(I32), pad_addresses[:, 0:E, :]))

        stats = sb("stats", [P, ST, 6])
        moments = sb("moments", [P, ST, 2])
        rstd = sb("rstd", [P, ST])
        newton = sb("newton", [P, 3, ST])
        R8 = [sb(f"route{i}", [P, ST, E]) for i in range(7)]
        choice_bf = sb("choice_bf", [P, ST, E], BF16)
        R1 = [sb(f"gatev{i}", [P, ST]) for i in range(10)]
        slot_i = [sb(f"slot{k}", [P, 2, ST], I32) for k in range(K)]
        scan = [sb(f"scan{i}", [P, 8 + ST, E]) for i in range(2)]
        base = [sb(f"base{i}", [P, E]) for i in range(2)]
        table_f = sb("table_f", [1, 8, NTILES])
        table_8 = sb("table_8", [1, 2, NTILES, E])
        counts_8 = sb("counts_8", [1, 6, 8 + E])
        counts_i = sb("counts_i", [1, 2, E], I32)
        table_i = [sb(f"table_i{n}", [1, 2, NTILES], I32) for n in range(2)]
        starts_i = [sb(f"starts_i{n}", [1, E], I32) for n in range(2)]
        for i in range(2):
            scans_zero = dve.did(dve_e.memset(scan[i][:], 0.0))
        counts_zero = dve.did(dve_e.memset(counts_8[:], 0.0))
        dve.need(scans_zero, counts_zero)

        def inverse_root(out, v, add, scratch, v_ready):
            a, y, z = (scratch[:, i, :] for i in range(3))
            dve.need(v_ready)
            m = dve.did(dve_e.tensor_scalar(a, v, add, None, ALU.add))
            dve.need(m)
            m = dve.did(dve_e.tensor_scalar(z.bitcast(I32), a.bitcast(I32), 1, None, ALU.logical_shift_right))
            dve.need(m)
            m = dve.did(dve_e.tensor_scalar(y.bitcast(I32), z.bitcast(I32), -1.0, float(0x5F3759DF), ALU.mult, ALU.add))
            for i in range(4):
                dve.need(m)
                m = dve.did(dve_e.tensor_tensor(z, y, y, ALU.mult))
                dve.need(m)
                m = dve.did(dve_e.scalar_tensor_tensor(z, z, -0.5, a, ALU.mult, ALU.mult))
                dve.need(m)
                m = dve.did(dve_e.scalar_tensor_tensor(out if i == 3 else y, z, 1.5, y, ALU.add, ALU.mult))
            return m

        def prepare(layer, s, xs_ready, state):
            rows = rows_ring.take()
            logits = psum.take()
            dve.need(*rows.freed)
            for q in range(ST // GT):
                g = s * (ST // GT) + q
                dve.need(*xs_ready(g))
                for j in range(GT * q, GT * q + GT):
                    m = dve.did(dve_e.bn_stats(stats[:, j, :], X[:, ST * s + j, :]))
                    dve.need(m)
                    m = dve.did(dve_e.bn_aggr(moments[:, j, :], stats[:, j, :]))
            m = inverse_root(rstd[:], moments[:, :, 1], LN_EPS, newton, m)
            dve.need(m)
            turned = []
            for q in range(ST // GT):
                g = s * (ST // GT) + q
                a, b = GT * q, GT * q + GT
                for j in range(a, b):
                    m = dve.did(dve_e.tensor_scalar(rows.ap[:, j, 0, 0:C], X[:, ST * s + j, :], moments[:, j, 0:1],
                                                    rstd[:, j:j + 1], ALU.subtract, ALU.mult))
                rows_ready = m
                dve.need(m)
                copied = dve.did(dve_e.tensor_copy(rows.ap[:, a:b, 1, 0:C], rows.ap[:, a:b, 0, 0:C]))
                bank = psum.take()
                pe.need(rows_ready, *bank.freed)
                for j in range(a, b):
                    m = pe_e.transpose(bank.ap[:, (j - a) * P:(j - a + 1) * P], rows.ap[:, j, 0, 0:C], ident)
                m = pe.did(m)
                act.need(m, *state["xT_free"].get(g, ()))
                m = act.did(act_e.activation(xT[:, GT * g:GT * g + GT, :].rearrange("p a b -> p (a b)"),
                                             bank.ap[:], ACT.Copy))
                psum.give(bank, m)
                turned.append(m)
                state["xT_ready"][g] = m
                yield
            pe.need(*logits.freed)
            for j in range(ST):
                if j % GT == 0:
                    pe.need(turned[j // GT])
                m = pe_e.matmul(logits.ap[:, j * E:(j + 1) * E], xT[:, ST * s + j, :],
                                gates[:, layer * E:(layer + 1) * E], start=True, stop=True)
            m = pe.did(m)
            yield
            L = logits.ap[:, 0:ST * E].rearrange("p (a b) -> p a b", b=E)
            score, m1, m2, less, tmp, place, tmp2 = (r[:] for r in R8)

            def over_e(a):
                return a.unsqueeze(2).to_broadcast([P, ST, E])

            def over_j(a):
                return a.unsqueeze(1).to_broadcast([P, ST, E])

            best, second, z, p1, p2, den, w1, w2, e2, sl = (r[:] for r in R1)

            def v(ins):
                m = dve.did(ins)
                dve.need(m)
                return m

            dve.need(m)
            v(dve_e.tensor_reduce(best, L, AX, ALU.max))
            v(dve_e.tensor_tensor(tmp, L, over_e(best), ALU.is_equal))
            v(dve_e.tensor_tensor(tmp, tmp, over_j(const("first")), ALU.mult))
            v(dve_e.tensor_reduce(second, tmp, AX, ALU.max))
            v(dve_e.tensor_tensor(m1, tmp, over_e(second), ALU.is_equal))
            v(dve_e.scalar_tensor_tensor(less, m1, -BIG, L, ALU.mult, ALU.add))
            v(dve_e.tensor_reduce(second, less, AX, ALU.max))
            v(dve_e.tensor_tensor(tmp, less, over_e(second), ALU.is_equal))
            v(dve_e.tensor_tensor(tmp, tmp, over_j(const("first")), ALU.mult))
            v(dve_e.tensor_reduce(e2, tmp, AX, ALU.max))
            v(dve_e.tensor_tensor(m2, tmp, over_e(e2), ALU.is_equal))
            chosen = v(dve_e.tensor_tensor(choice_bf[:], m1, m2, ALU.add))
            shifted = v(dve_e.tensor_tensor(score, L, over_e(best), ALU.subtract))
            psum.give(logits, shifted)
            act.need(shifted)
            exps = act.did(act_e.activation(score, score, ACT.Exp))
            ranks = psum.take()
            pe.need(chosen, *ranks.freed)
            flat = choice_bf[:].rearrange("p a b -> p (a b)")
            pe_e.matmul(ranks.ap[:, 0:ST * E], before_bf[:], flat, start=True, stop=True)
            m = pe.did(pe_e.matmul(ranks.ap[:, ST * E:2 * ST * E], ones_bf[:], flat, start=True, stop=True))
            yield
            dve.need(m)
            v(dve_e.tensor_copy(scan[0][:, 8:, :], ranks.ap[:, ST * E:2 * ST * E].rearrange("p (a b) -> p a b", b=E)))
            for i, d in enumerate((1, 2, 4, 8)):
                a, b = scan[i % 2], scan[(i + 1) % 2]
                v(dve_e.tensor_tensor(b[:, 8:, :], a[:, 8:, :], a[:, 8 - d:8 + ST - d, :], ALU.add))
            v(dve_e.tensor_tensor(place, ranks.ap[:, 0:ST * E].rearrange("p (a b) -> p a b", b=E),
                                  scan[0][:, 7:7 + ST, :], ALU.add))
            psum.give(ranks, (dve.sem, dve.n))
            old = const("regions") if s == 0 else base[s % 2][:]
            v(dve_e.tensor_tensor(place, place, over_j(old), ALU.add))
            v(dve_e.tensor_tensor(base[(s + 1) % 2][:], old, scan[0][:, 7 + ST, :], ALU.add))
            for k, mk in enumerate((m1, m2)):
                v(dve_e.tensor_tensor(tmp, place, mk, ALU.mult))
                v(dve_e.tensor_reduce(sl, tmp, AX, ALU.add))
                placed = v(dve_e.tensor_copy(slot_i[k][:, s % 2, :], sl))
            dve.need(exps)
            v(dve_e.tensor_reduce(z, score, AX, ALU.add))
            v(dve_e.reciprocal(p1, z))
            v(dve_e.tensor_tensor(tmp2, score, m2, ALU.mult))
            v(dve_e.tensor_reduce(e2, tmp2, AX, ALU.add))
            v(dve_e.tensor_tensor(p2, e2, p1, ALU.mult))
            v(dve_e.scalar_tensor_tensor(den, p1, GATE_EPS if layer == 0 else 0.0, p2, ALU.add, ALU.add))
            v(dve_e.reciprocal(sl, den))
            dve.did(dve_e.tensor_tensor(rows.ap[:, :, 0, C + 1], p1, sl, ALU.mult))
            dve.did(dve_e.tensor_tensor(rows.ap[:, :, 1, C + 1], p2, sl, ALU.mult))
            for k in range(K):
                filled = dve.did(dve_e.tensor_copy(rows.ap[:, :, k, C].bitcast(I32),
                                                   addresses[:, k, ST * s:ST * s + ST]))
            yield
            pool.need(placed, filled)
            for j in range(ST):
                for k in range(K):
                    m = rows.arrival.by(pool_e.indirect_dma_start(
                        out=sent, out_offset=bass.IndirectOffsetOnAxis(ap=slot_i[k][:, s % 2, j:j + 1], axis=0),
                        in_=rows.ap[:, j, k, :], in_offset=None))
                if j % 4 == 3:
                    yield
            state["sent"][s % 2] = m
            rows_ring.give(rows, m)

        def plan(layer, state):
            last = base[NS % 2]

            def v(ins):
                m = dve.did(ins)
                dve.need(m)
                return m

            n, up, c0, c1, nt, _ = (counts_8[:, i, 8:] for i in range(6))
            v(dve_e.tensor_copy(starts_i[layer][:], last[0:1, :]))
            v(dve_e.tensor_tensor(n, last[0:1, :], const("regions")[0:1, :], ALU.subtract))
            v(dve_e.tensor_scalar(counts_i[:, 0, :], n, float(SLOTS - 1), None, ALU.add))
            v(dve_e.tensor_scalar(counts_i[:, 1, :], counts_i[:, 0, :], SLOTS.bit_length() - 1, None,
                                  ALU.logical_shift_right))
            v(dve_e.tensor_copy(nt, counts_i[:, 1, :]))
            v(dve_e.tensor_copy(c0, nt))
            for i, d in enumerate((1, 2, 4)):
                a, b = 2 + i % 2, 2 + (i + 1) % 2
                v(dve_e.tensor_tensor(counts_8[:, b, 8:], counts_8[:, a, 8:], counts_8[:, a, 8 - d:8 + E - d], ALU.add))
            ends = counts_8[:, 3, 8:]
            tiles = const("tiles")[0:1, :]
            past, mine = table_8[:, 0, :, :], table_8[:, 1, :, :]
            shape = [1, NTILES, E]
            v(dve_e.tensor_tensor(past, tiles.unsqueeze(2).to_broadcast(shape),
                                  ends.unsqueeze(1).to_broadcast(shape), ALU.is_ge))
            v(dve_e.tensor_tensor(mine, past, nt.unsqueeze(1).to_broadcast(shape), ALU.mult))
            f = [table_f[:, i, :] for i in range(8)]
            v(dve_e.tensor_reduce(f[0], past, AX, ALU.add))
            v(dve_e.tensor_reduce(f[1], mine, AX, ALU.add))
            v(dve_e.tensor_tensor(f[2], tiles, f[1], ALU.subtract))
            v(dve_e.tensor_scalar(f[3], f[0], float(REGION), None, ALU.mult))
            v(dve_e.scalar_tensor_tensor(f[4], f[2], float(SLOTS), f[3], ALU.mult, ALU.add))
            v(dve_e.tensor_copy(table_i[layer][:, 1, :], f[4]))
            m = v(dve_e.tensor_scalar(table_i[layer][:, 0, :], f[0], float(E - 1), None, ALU.min))
            sp.need(m, pads_ready)
            for e in range(E):
                r = sp_e.value_load(starts_i[layer][0:1, e:e + 1], min_val=0, max_val=DUMMY - SLOTS)
                pad_arrival.by(sp_e.dma_start(sent[bass.ds(r, SLOTS), :].rearrange("(s p) c -> p s c", p=P), pads[:, e, :, :]))

        def attention0(g, state):
            xg = xT[:, GT * g:GT * g + GT, :]
            pe.need(state["xT_ready"][g])
            q_ps = psum.take()
            pe.need(*q_ps.freed)
            m_q = pe.did(pe_e.matmul(q_ps.ap[:], w_attn0[:, 0:C], xg.rearrange("p a b -> p (a b)"), start=True, stop=True))
            kv_ps, m_kv = [], []
            for h in range(2):
                bank = psum.take()
                pe.need(*bank.freed)
                for i in range(2):
                    o = bank.ap[:, 2 * C * i:2 * C * (i + 1)]
                    pe_e.matmul(o, xg[:, 2 * h + i, :], w_attn0[:, C:3 * C], start=True, stop=False)
                    m = pe_e.matmul(o, ones[:], brow[:, 0:2 * C], start=False, stop=True)
                kv_ps.append(bank)
                m_kv.append(pe.did(m))
            yield
            q, q_e = big.take(), big.take()
            act.need(m_q, *q_e.freed)
            m = act.did(act_e.activation(q_e.ap[:], q_ps.ap[:], ACT.Exp, bias=cols[:, 0:1]))
            dve.need(m)
            m = dve.did(dve_e.tensor_scalar(q_e.ap[:], q_e.ap[:], 1.0, None, ALU.min))
            dve.need(m, *q.freed)
            q_ready = dve.did(dve_e.scalar_tensor_tensor(q.ap[:], q_ps.ap[:], bq0p1[:], q_e.ap[:], ALU.add, ALU.max))
            psum.give(q_ps, q_ready)
            big.give(q_e, q_ready)
            k, k_e, v = big.take(), big.take(), big.take()
            k_ready, v_ready = [], []
            for h in range(2):
                src = kv_ps[h].ap[:].rearrange("p (a b) -> p a b", b=2 * C)
                c0, c1 = 2 * C * h, 2 * C * (h + 1)

                def half(s):
                    return s.ap[:, c0:c1].rearrange("p (a b) -> p a b", b=C)

                act.need(m_kv[h], *k_e.freed)
                m = act.did(act_e.activation(half(k_e), src[:, :, 0:C], ACT.Exp))
                act.need(*v.freed)
                v_ready.append(act.did(act_e.activation(half(v), src[:, :, C:2 * C], ACT.Copy)))
                dve.need(m)
                m = dve.did(dve_e.tensor_scalar(half(k_e), half(k_e), 1.0, None, ALU.min))
                dve.need(m, v_ready[h], *k.freed)
                k_ready.append(dve.did(dve_e.scalar_tensor_tensor(half(k), src[:, :, 0:C], 1.0, half(k_e), ALU.add, ALU.max)))
                psum.give(kv_ps[h], k_ready[h])
            big.give(k_e, *k_ready)
            yield
            kv_bank = psum.take()
            pe.need(*kv_bank.freed)
            masks = []
            for h in range(2):
                pe.need(k_ready[h], v_ready[h])
                for i in range(2):
                    sl = slice((2 * h + i) * C, (2 * h + i + 1) * C)
                    m = pe_e.matmul(kv_bank.ap[:, h * P:(h + 1) * P], v.ap[:, sl], k.ap[:, sl], start=(i == 0), stop=(i == 1))
            m = pe.did(m)
            big.give(k, m)
            big.give(v, m)
            kvT = big.take()
            dve.need(m, *kvT.freed)
            m = dve.did(dve_e.tensor_tensor(kvT.ap[:, 0:2 * P].rearrange("p (a b) -> p a b", b=P),
                                            kv_bank.ap[:, 0:2 * P].rearrange("p (a b) -> p a b", b=P),
                                            const("heads0").unsqueeze(1).to_broadcast([P, 2, P]), ALU.mult))
            psum.give(kv_bank, m)
            yield
            mix_bank = psum.take()
            pe.need(m, *mix_bank.freed)
            for h in range(2):
                m = pe_e.matmul(mix_bank.ap[:, h * C:(h + 1) * C], kvT.ap[:, h * P:(h + 1) * P], w_attn0[:, 3 * C:4 * C],
                                start=True, stop=True)
            m = pe.did(m)
            big.give(kvT, m)
            mix = big.take()
            act.need(m, *mix.freed)
            m = act.did(act_e.activation(mix.ap[:, 0:2 * C], mix_bank.ap[:, 0:2 * C], ACT.Copy))
            psum.give(mix_bank, m)
            yield
            y = psum.take()
            pe.need(q_ready, m, *y.freed)
            for i in range(GT):
                o = y.ap[:, i * C:(i + 1) * C]
                pe_e.matmul(o, q.ap[:, i * P:(i + 1) * P], mix.ap[:, (i // 2) * C:(i // 2 + 1) * C], start=True, stop=False)
                m = pe_e.matmul(o, ones[:], brow[:, 2 * C:3 * C], start=False, stop=True)
            m = pe.did(m)
            big.give(q, m)
            big.give(mix, m)
            xr = X[:, GT * g:GT * g + GT, :].rearrange("p a b -> p (a b)")
            dve.need(m)
            m = dve.did(dve_e.tensor_tensor(xr, xr, y.ap[:], ALU.add))
            psum.give(y, m)
            state["X_done"][g] = m

        def shared(g, state):
            xg = xT[:, GT * g:GT * g + GT, :].rearrange("p a b -> p (a b)")
            pe.need(state["xT_ready"][g])
            h = []
            for c0, n in FSC:
                gate, up = psum.take(), psum.take()
                pe.need(*gate.freed)
                m_g = pe.did(pe_e.matmul(gate.ap[0:n, :], w_shared[:, c0:c0 + n], xg, start=True, stop=True))
                pe.need(*up.freed)
                m_u = pe.did(pe_e.matmul(up.ap[0:n, :], w_shared[:, FS + c0:FS + c0 + n], xg, start=True, stop=True))
                s, hc = big.take(), big.take()
                act.need(m_g, *s.freed)
                m = act.did(act_e.activation(s.ap[0:n, :], gate.ap[0:n, :], ACT.Silu))
                psum.give(gate, m)
                dve.need(m, m_u, *hc.freed)
                m = dve.did(dve_e.tensor_tensor(hc.ap[0:n, :], s.ap[0:n, :], up.ap[0:n, :], ALU.mult))
                psum.give(up, m)
                big.give(s, m)
                h.append((hc, m, n))
                yield
            state["xT_free"][g] = (m_u,)
            y = psum.take()
            pe.need(*y.freed, *(m for _, m, _ in h))
            for i in range(GT):
                for c, (hc, _, n) in enumerate(h):
                    m = pe_e.matmul(y.ap[:, i * C:(i + 1) * C], hc.ap[0:n, i * P:(i + 1) * P],
                                    w_shared[0:n, 2 * FS + c * C:2 * FS + (c + 1) * C], start=(c == 0), stop=(c == 2))
            m = pe.did(m)
            for hc, _, _ in h:
                big.give(hc, m)
            xr = X[:, GT * g:GT * g + GT, :].rearrange("p a b -> p (a b)")
            dve.need(m, state["X_done"][g])
            m = dve.did(dve_e.tensor_tensor(xr, xr, y.ap[:], ALU.add))
            psum.give(y, m)
            state["X_done"][g] = m

        WCOLS = max(W0COLS, W1COLS)
        arena = sb("arena", [P, 3 * WCOLS])
        stage = Ring([Slot(arena[:, n * WCOLS:(n + 1) * WCOLS], Arrival(sem(f"stage{n}_dma"))) for n in range(3)])
        tile_in = ring("tile_in", 4, [P, SUB, ROW], dma=True)
        tile_out = ring("tile_out", 3, [P, SUB, C], dma=True)
        return_marks = {}

        def fetch(layer, n, state):
            w, r = stage.take(), tile_in.take()
            if n == 0:
                sp.need(*state["sent"], pad_arrival.all, *state["X_done"].values())
            ncols = (W0COLS, W1COLS)[layer]
            e = sp_e.value_load(table_i[layer][0:1, 0, n:n + 1], min_val=0, max_val=E - 1)
            first = sp_e.value_load(table_i[layer][0:1, 1, n:n + 1], min_val=0, max_val=DUMMY + (NDUMMY - 1) * SLOTS)
            sp.need(*w.freed)
            w_here = w.arrival.by(sp_e.dma_start(
                w.ap[:, 0:ncols], t[f"experts{layer}"][bass.ds(e, 1), :, :].rearrange("a p n -> p (a n)")))
            sp.need(*r.freed)
            r_here = r.arrival.by(sp_e.dma_start(
                r.ap[:], sent[bass.ds(first, SLOTS), :].rearrange("(s p) c -> p s c", p=P)))
            return w, r, w_here, r_here

        def expert_tile(layer, n, state):
            w, r, w_here, r_here = fetch(layer, n, state)
            yield
            bank = psum.take()
            pe.need(r_here, *bank.freed)
            for i in range(SUB):
                m = pe_e.transpose(bank.ap[:, i * P:(i + 1) * P], r.ap[:, i, 0:C], ident)
            m = pe.did(m)
            x = big.take()
            dve.need(m, *x.freed)
            m = dve.did(dve_e.tensor_copy(x.ap[:], bank.ap[:]))
            psum.give(bank, m)
            x_ready = m
            yield
            pe.need(w_here, x_ready)
            h = []
            if layer == 0:
                gate, up, tail = psum.take(), psum.take(), psum.take()
                pe.need(*gate.freed)
                m_g = pe.did(pe_e.matmul(gate.ap[:], w.ap[:, 0:P], x.ap[:], start=True, stop=True))
                pe.need(*up.freed)
                m_u = pe.did(pe_e.matmul(up.ap[:], w.ap[:, F0P + 64:2 * F0P], x.ap[:], start=True, stop=True))
                pe.need(*tail.freed)
                m_t = pe.did(pe_e.matmul(tail.ap[:], w.ap[:, P:2 * P], x.ap[:], start=True, stop=True))
                big.give(x, m_t)
                for n_h, src_g, src_u, m1, m2, slots in ((P, gate.ap, up.ap, m_g, m_u, (gate, up)),
                                                         (F0T, tail.ap, tail.ap[64:64 + F0T, :], m_t, m_t, (tail,))):
                    s, hc = big.take(), big.take()
                    act.need(m1, *s.freed)
                    m = act.did(act_e.activation(s.ap[0:n_h, :], src_g[0:n_h, :], ACT.Silu))
                    dve.need(m, m2, *hc.freed)
                    m = dve.did(dve_e.tensor_tensor(hc.ap[0:n_h, :], s.ap[0:n_h, :], src_u[0:n_h, :], ALU.mult))
                    for slot in slots:
                        psum.give(slot, m)
                    big.give(s, m)
                    h.append((hc, m, n_h))
                down, b1, b2 = 2 * F0P, None, None
            else:
                b1 = F1 + NC1 * C
                b2 = b1 + NC1
                down = F1
                for c in range(NC1):
                    z = psum.take()
                    pe.need(*z.freed)
                    m = pe.did(pe_e.matmul(z.ap[:], w.ap[:, c * P:(c + 1) * P], x.ap[:], start=True, stop=True))
                    hc = big.take()
                    act.need(m, w_here, *hc.freed)
                    m1 = act.did(act_e.activation(hc.ap[:], z.ap[:], ACT.Gelu, bias=w.ap[:, b1 + c:b1 + c + 1]))
                    psum.give(z, m1)
                    h.append((hc, m1, P))
                big.give(x, m)
            yield
            y = psum.take()
            pe.need(*y.freed, *(m for _, m, _ in h))
            for i in range(SUB):
                for c, (hc, _, k) in enumerate(h):
                    m = pe_e.matmul(y.ap[:, i * C:(i + 1) * C], hc.ap[0:k, i * P:(i + 1) * P],
                                    w.ap[0:k, down + c * C:down + (c + 1) * C], start=(c == 0), stop=(c == len(h) - 1))
            m_y = pe.did(m)
            for hc, _, _ in h:
                big.give(hc, m_y)
            o = tile_out.take()
            src = y.ap[:].rearrange("p (a b) -> p a b", b=C)
            dve.need(m_y, r_here, *o.freed)
            if layer == 1:
                dve.need(w_here)
                m = dve.did(dve_e.tensor_tensor(o.ap[:], src, w.ap[:, b2:b2 + C].unsqueeze(1).to_broadcast([P, SUB, C]), ALU.add))
                dve.need(m)
                psum.give(y, m)
                src = o.ap[:]
            m = dve.did(dve_e.tensor_tensor(o.ap[:], src, r.ap[:, :, C + 1:C + 2].to_broadcast([P, SUB, C]), ALU.mult))
            if layer == 0:
                psum.give(y, m)
            stage.give(w, m_y, m)
            yield
            pool.need(m)
            for i in range(SUB):
                m = o.arrival.by(pool_e.indirect_dma_start(
                    out=back, out_offset=bass.IndirectOffsetOnAxis(ap=r.ap[:, i, C:C + 1].bitcast(I32), axis=0),
                    in_=o.ap[:, i, :], in_offset=None))
            tile_out.give(o, m)
            tile_in.give(r, m)
            return_marks[o.arrival.sem.name] = m

        def collect(g, state, to=None):
            sp.need(*return_marks.values())
            parts = []
            for k in range(K):
                part = joined.take()
                sp.need(*part.freed)
                rows = slice(k * TOK + g * GT * P, k * TOK + (g + 1) * GT * P)
                parts.append((part, part.arrival.by(sp_e.dma_start(
                    part.ap[:], back[rows, :].rearrange("(s p) c -> p s c", p=P)))))
            yield
            xr = X[:, GT * g:GT * g + GT, :]
            for part, here in parts:
                dve.need(here, state["X_done"][g])
                m = dve.did(dve_e.tensor_tensor(xr, xr, part.ap[:], ALU.add))
                joined.give(part, m)
                state["X_done"][g] = m

        joined = ring("joined", 4, [P, GT, C], dma=True)

        def attention1(g, state):
            xg = xT[:, GT * g:GT * g + GT, :]
            flat = xg.rearrange("p a b -> p (a b)")
            pe.need(state["xT_ready"][g])
            z_ps = []
            for c in range(2):
                bank = psum.take()
                pe.need(*bank.freed)
                z_ps.append((bank, pe.did(pe_e.matmul(bank.ap[:], w_attn1[:, c * C:(c + 1) * C], flat, start=True, stop=True))))
            vu_ps = []
            for h in range(2):
                bank = psum.take()
                pe.need(*bank.freed)
                for i in range(2):
                    o = bank.ap[:, 2 * C * i:2 * C * (i + 1)]
                    pe_e.matmul(o, xg[:, 2 * h + i, :], w_attn1[:, 2 * C:4 * C], start=True, stop=False)
                    m = pe_e.matmul(o, ones[:], brow[:, 3 * C:5 * C], start=False, stop=True)
                vu_ps.append((bank, pe.did(m)))
            state["xT_free"][g] = (vu_ps[-1][1],)
            yield
            q, k = big.take(), big.take()
            ready = []
            for c, dst in ((0, q), (1, k)):
                bank, m_z = z_ps[c]
                e = big.take()
                act.need(m_z, *e.freed)
                m = act.did(act_e.activation(e.ap[:], bank.ap[:], ACT.Exp, bias=cols[:, 1 + c:2 + c]))
                dve.need(m)
                m = dve.did(dve_e.tensor_scalar(e.ap[:], e.ap[:], 1.0, -1.0, ALU.min, ALU.add))
                dve.need(m, *dst.freed)
                m = dve.did(dve_e.scalar_tensor_tensor(dst.ap[:], bank.ap[:], cols[:, 1 + c:2 + c], e.ap[:], ALU.add, ALU.max))
                psum.give(bank, m)
                big.give(e, m)
                ready.append(m)
            q_ready, k_ready = ready
            kh = [big.take() for _ in range(HEADS32)]
            kh_ready = []
            for s in range(HEADS32):
                dve.need(k_ready, *kh[s].freed)
                kh_ready.append(dve.did(dve_e.tensor_scalar(kh[s].ap[:], k.ap[:], const("parity")[:, s:s + 1], None, ALU.mult)))
            vu, th = bigger.take(), big.take()
            vu_ready = []
            for h in range(2):
                bank, m_z = vu_ps[h]
                act.need(m_z, *th.freed)
                m = act.did(act_e.activation(th.ap[:], bank.ap[:], ACT.Tanh, scale=0.5))
                dve.need(m, *vu.freed)
                m = dve.did(dve_e.scalar_tensor_tensor(vu.ap[:, 512 * h:512 * (h + 1)], th.ap[:], 1.0, bank.ap[:], ALU.add, ALU.mult))
                psum.give(bank, m)
                th.freed = (m,)
                vu_ready.append(m)
            big.give(th, m)
            yield
            bank = psum.take()
            pe.need(k_ready, *bank.freed)
            for h in range(2):
                m = pe_e.transpose(bank.ap[:, h * P:(h + 1) * P], k.ap[:, 2 * h * P:(2 * h + 1) * P], ident)
            m = pe.did(m)
            k_tok = small2.take()
            act.need(m, *k_tok.freed)
            k_tok_ready = act.did(act_e.activation(k_tok.ap[:], bank.ap[:, 0:2 * P], ACT.Copy))
            psum.give(bank, k_tok_ready)
            big.give(k, m)
            att_bank = psum.take()
            att = bigger_e.take()

            def energies(h):
                for j in range(H1 // HEADS32):
                    bank = psum.take()
                    pe.need(q_ready, *kh_ready, *bank.freed)
                    for i in range(2):
                        for s in range(HEADS32):
                            tok = slice((2 * h + i) * P, (2 * h + i + 1) * P)
                            m = pe_e.matmul(bank.ap[:, (2 * i + s) * P:(2 * i + s + 1) * P],
                                            kh[s].ap[32 * j:32 * j + 32, tok], q.ap[32 * j:32 * j + 32, tok],
                                            start=True, stop=True)
                    m = pe.did(m)
                    dve.need(m, *(att.freed if h == 0 else state["att_used"]))
                    m = dve.did(dve_e.tensor_tensor(att.ap[:, j, :].rearrange("p (a b) -> p a b", b=P),
                                                    bank.ap[:].rearrange("p (a b) -> p a b", b=P),
                                                    const("causal").unsqueeze(1).to_broadcast([P, 4, P]), ALU.mult))
                    psum.give(bank, m)
                return m

            outs = []
            for h in range(2):
                masked = energies(h)
                kv_bank = psum.take()
                pe.need(k_tok_ready, vu_ready[h], *kv_bank.freed)
                m = pe.did(pe_e.matmul(kv_bank.ap[:, 0:C], k_tok.ap[:, h * P:(h + 1) * P], vu.ap[:, 512 * h:512 * h + C],
                                       start=True, stop=True))
                kv = small.take()
                dve.need(m, *kv.freed)
                kv_ready = dve.did(dve_e.tensor_tensor(kv.ap[:], kv_bank.ap[:, 0:C], const("heads1"), ALU.mult))
                psum.give(kv_bank, kv_ready)
                if h == 1:
                    small2.give(k_tok, m)
                yield
                pe.need(masked, kv_ready)
                if h == 0:
                    pe.need(*att_bank.freed)
                for i in range(2):
                    tile = 2 * h + i
                    o0 = tile * C
                    if i == 1:
                        pe_e.matmul(att_bank.ap[:, o0:o0 + C], q.ap[:, tile * P:(tile + 1) * P], kv.ap[:],
                                    start=False, stop=False, skip_group_check=True)
                    for head in range(H1):
                        j, s = divmod(head, HEADS32)
                        m = pe_e.matmul(att_bank.ap[:, o0 + head * D1:o0 + (head + 1) * D1],
                                        att.ap[:, j, (2 * i + s) * P:(2 * i + s + 1) * P],
                                        vu.ap[:, 512 * h + 256 * i + head * D1:512 * h + 256 * i + (head + 1) * D1],
                                        start=(tile == 0 and head == 0), stop=(tile == GT - 1 and head == H1 - 1),
                                        skip_group_check=True)
                m = pe.did(m)
                state["att_used"] = (m,)
                small.give(kv, m)
            att_done = m
            bigger_e.give(att, m)
            big.give(q, m)
            for s in kh:
                big.give(s, m)
            sq, uo, ss = big.take(), big.take(), sums.take()
            act.need(att_done, *sq.freed, *ss.freed)
            for i in range(GT):
                m_sq = act.did(act_e.activation(sq.ap[:, i * C:(i + 1) * C], att_bank.ap[:, i * C:(i + 1) * C], ACT.Square,
                                                accum_out=ss.ap[:, 3, i:i + 1]))
            big.give(sq, m_sq)
            dve.need(m_sq, *uo.freed)
            m = dve.did(dve_e.tensor_tensor(uo.ap[:].rearrange("p (a b) -> p a b", b=C),
                                            att_bank.ap[:].rearrange("p (a b) -> p a b", b=C),
                                            vu.ap[:].rearrange("p (a b) -> p a b", b=2 * C)[:, :, C:2 * C], ALU.mult))
            psum.give(att_bank, m, m_sq)
            bigger.give(vu, m)
            uo_ready = m
            tot = ss.ap[:, 3, :]
            m = inverse_root(ss.ap[:, 4, :], tot, 0.0, ss.ap[:, 0:3, :], m_sq)
            dve.need(m)
            m = dve.did(dve_e.tensor_tensor(ss.ap[:, 0, :], tot, ss.ap[:, 4, :], ALU.mult))
            dve.need(m)
            m = dve.did(dve_e.tensor_scalar(ss.ap[:, 1, :], ss.ap[:, 0, :], float(C) ** -0.5, RMS_EPS, ALU.mult, ALU.add))
            dve.need(m)
            inv_ready = dve.did(dve_e.reciprocal(ss.ap[:, 5, :], ss.ap[:, 1, :]))
            yield
            bank = psum.take()
            pe.need(uo_ready, *bank.freed)
            for i in range(GT):
                m = pe_e.transpose(bank.ap[:, i * P:(i + 1) * P], uo.ap[:, i * C:(i + 1) * C], ident)
            m = pe.did(m)
            big.give(uo, m)
            uoT = big.take()
            act.need(m, *uoT.freed)
            m = act.did(act_e.activation(uoT.ap[:], bank.ap[:], ACT.Copy))
            psum.give(bank, m)
            yield
            y = psum.take()
            pe.need(m, *y.freed)
            for i in range(GT):
                m = pe_e.matmul(y.ap[:, i * C:(i + 1) * C], uoT.ap[:, i * P:(i + 1) * P], wo1s[:], start=True, stop=True)
            m_y = pe.did(m)
            big.give(uoT, m_y)
            xr = X[:, GT * g:GT * g + GT, :]
            dve.need(state["X_done"][g], state["rows_done"][g // (ST // GT)])
            m = dve.did(dve_e.tensor_tensor(xr, xr, bo1[:].unsqueeze(1).to_broadcast([P, GT, C]), ALU.add))
            dve.need(m, m_y, inv_ready)
            for i in range(GT):
                m = dve.did(dve_e.scalar_tensor_tensor(X[:, GT * g + i, :], y.ap[:, i * C:(i + 1) * C], ss.ap[:, 5, i:i + 1],
                                                       X[:, GT * g + i, :], ALU.mult, ALU.add))
            psum.give(y, m)
            sums.give(ss, m)
            state["X_done"][g] = m

        n_energy = H1 // HEADS32 * 512
        bigger = Ring([Slot(arena[:, n_energy:n_energy + 4 * 2 * C]), Slot(sb("bigger", [P, 4 * 2 * C]))])
        bigger_e = Ring([Slot(arena[:, 0:n_energy].rearrange("p (a b) -> p a b", b=512))])
        small2 = ring("small2", 2, [P, 2 * P])
        sums = ring("sums", 3, [P, 6, GT])

        L0 = {"xT_ready": {}, "xT_free": {}, "X_done": {}, "sent": [None, None], "rows_done": {}}
        gps = ST // GT

        def attention_set(fn, s, state):
            for q in range(gps):
                yield from fn(s * gps + q, state)

        def run_together(*works):
            works = [w for w in works if w is not None]
            while works:
                works = [w for w in works if next(w, "done") != "done"]

        def pipelined(fn, groups, state, depth=2):
            groups = iter(groups)
            active = []
            while True:
                if len(active) < depth:
                    g = next(groups, None)
                    if g is not None:
                        active.append(fn(g, state))
                if not active:
                    return
                active = [w for w in active if next(w, "done") != "done"]
                yield

        for s in range(NS + 1):
            run_together(
                prepare(0, s, lambda g: (x_here[g // gps],), L0) if s < NS else None,
                pipelined(attention0, range((s - 1) * gps, s * gps), L0) if s else None)
        plan(0, L0)
        in_turn([shared(g, L0) for g in range(NG)], 1)
        in_turn([expert_tile(0, n, L0) for n in range(NTILES)], 3)

        L1 = {"xT_ready": {}, "xT_free": L0["xT_free"], "X_done": L0["X_done"], "sent": [None, None], "rows_done": {},
              "att_used": ()}

        def set1(s):
            for q in range(gps):
                yield from collect(s * gps + q, L1)
            yield from prepare(1, s, lambda g: (L1["X_done"][g],), L1)

        def mark_rows(s):
            L1["rows_done"][s] = (dve.sem, dve.n)

        for s in range(NS + 1):
            run_together(
                set1(s) if s < NS else None,
                pipelined(attention1, range((s - 1) * gps, s * gps), L1, 1) if s else None)
            mark_rows(s)
        plan(1, L1)
        in_turn([expert_tile(1, n, L1) for n in range(NTILES)], 3)

        out_arrival = Arrival(sem("out_dma"))
        y_out = out.rearrange("(n p) c -> p n c", p=P)

        def finish(g, state):
            yield from collect(g, state)
            act.need(state["X_done"][g])
            out_arrival.by(act_e.dma_start(y_out[:, GT * g:GT * g + GT, :], X[:, GT * g:GT * g + GT, :]))

        in_turn([finish(g, L1) for g in range(NG)], 2)
        act.need(out_arrival.all)


def kernel(**inputs):
    import concourse.bacc as bacc
    from concourse.bass_utils import run_bass_kernel_spmd

    i = {k: np.asarray(v) for k, v in inputs.items()}

    def padded(a, n):
        return np.concatenate([a, np.zeros((*a.shape[:-1], n - a.shape[-1]), a.dtype)], axis=-1)

    def padded_rows(a, n):
        return np.concatenate([a, np.zeros((*a.shape[:-2], n - a.shape[-2], a.shape[-1]), a.dtype)], axis=-2)

    wd = padded_rows(i["L0_ffn_wd"], 2 * P)
    wu = i["L0_ffn_wu"]
    experts0 = np.concatenate([padded(i["L0_ffn_wg"], F0P), padded(wu[:, :, P:], 64), wu[:, :, 0:P], wd[:, 0:P], wd[:, P:2 * P]], axis=2)
    w2 = i["L1_ffn_w2"].reshape(E, NC1, P, C).transpose(0, 2, 1, 3).reshape(E, P, NC1 * C)
    b1 = i["L1_ffn_b1"].reshape(E, NC1, P).transpose(0, 2, 1)
    b2 = np.broadcast_to(i["L1_ffn_b2"][:, None, :], (E, P, C))
    experts1 = np.concatenate([i["L1_ffn_w1"], w2, b1, b2], axis=2)
    swd = padded_rows(i["L0_ffn_swd"], 3 * P)
    arrays = {
        "x": i["L0_attn_x"].reshape(TOK, C),
        "consts": constants()[0],
        "addresses": return_addresses(),
        "pad_addresses": padding_addresses(),
        "gates": np.concatenate([i["L0_ffn_gate_w"].T, i["L1_ffn_w_router"].T], axis=1),
        "cols": np.stack([i["L0_attn_bq"], i["L1_attn_bq"], i["L1_attn_bk"], i["L1_attn_scale"], i["L1_attn_scale"]], axis=1),
        "brow": np.concatenate([i["L0_attn_bk"], i["L0_attn_bv"], i["L0_attn_bo"], i["L1_attn_bv"], i["L1_attn_bu"]])[None, :],
        "w_attn0": np.concatenate([i[f"L0_attn_W{n}"].T for n in "qkvo"], axis=1),
        "w_attn1": np.concatenate([i[f"L1_attn_W{n}"].T for n in "qkvuo"], axis=1),
        "w_shared": np.concatenate([i["L0_ffn_swg"], i["L0_ffn_swu"], swd[0:P], swd[P:2 * P], swd[2 * P:3 * P]], axis=1),
        "bo1": np.broadcast_to(i["L1_attn_bo"][None, :], (P, C)),
        "experts0": experts0,
        "experts1": experts1,
    }
    nc = bacc.Bacc("TRN2", target_bir_lowering=False, num_devices=1)
    feed, t = {}, {}
    for name, a in arrays.items():
        a = np.ascontiguousarray(a)
        feed[f"in_{name}"] = a
        t[name] = nc.dram_tensor(f"in_{name}", a.shape, mybir.dt.from_np(a.dtype), kind="ExternalInput").ap()
    out = nc.dram_tensor("out", (TOK, C), F32, kind="ExternalOutput").ap()
    build(nc, t, out)
    r = run_bass_kernel_spmd(nc, [feed], core_ids=[0])
    return r.results[0]["out"].reshape(B, S, C)
```

```python
from collections import deque
from contextlib import ExitStack

import concourse.bass as bass
import numpy as np
from concourse import mybir
from concourse.alu_op_type import AluOpType as ALU

F32 = mybir.dt.float32
I32 = mybir.dt.int32
BF16 = mybir.dt.bfloat16
ACT = mybir.ActivationFunctionType
AX = mybir.AxisListType.X

P = 128
B, S, C = 32, 256, 128
TOK = B * S
NT = TOK // P
GT = 4
NG = NT // GT
ST = 16
NS = NT // ST
gps = ST // GT
E = 8
K = 2
SLOTS = 512
SUB = SLOTS // P
NTILES = (K * TOK - E) // SLOTS + E
REGION = TOK + SLOTS
DUMMY = E * REGION
NDUMMY = NTILES - K * TOK // SLOTS
ROW = C + 2
TRASH = K * TOK
NPAD = E + NDUMMY
H0, D0 = 16, 8
H1, D1 = 8, 16
HEADS32 = 32 // D1
HEADS64 = 64 // D1
F0 = 176
F0P = 192
F0T = F0 - P
FS = 352
FSC = [(0, 128), (128, 128), (256, 96)]
F1 = 512
NC1 = F1 // P
W0COLS = 2 * F0P + 2 * C
W1COLS = F1 + NC1 * C + NC1 + C
LN_EPS = 1e-5
RMS_EPS = 1e-8
GATE_EPS = 1e-20
BIG = 3.0e38


def constants():
    p = np.arange(P)
    blocks = {
        "ident": np.eye(P),
        "before": p[:, None] < p[None, :],
        "causal": 0.5 * (p[:, None] <= p[None, :]),
        "heads0": p[:, None] // D0 == p[None, :] // D0,
        "heads1": 0.5 * (p[:, None] // D1 == p[None, :] // D1),
        "head_of_64": (p[:, None] // D1) % HEADS64 == np.arange(HEADS64)[None, :],
        "first": np.broadcast_to(E - np.arange(E), (P, E)),
        "regions": np.broadcast_to(np.arange(E) * REGION, (P, E)),
        "tiles": np.broadcast_to(np.arange(NTILES), (P, NTILES)),
    }
    at, cols = {}, 0
    for name, block in blocks.items():
        at[name] = (cols, block.shape[1])
        cols += block.shape[1]
    return np.concatenate([b.astype(np.float32) for b in blocks.values()], axis=1), at


def return_addresses():
    token = np.arange(NT)[None, :] * P + np.arange(P)[:, None]
    return np.stack([token + k * TOK for k in range(K)], axis=1).astype(np.int32)


def padding_addresses():
    n = np.arange(NPAD * SUB).reshape(1, NPAD, SUB)
    return (TRASH + n * P + np.arange(P).reshape(P, 1, 1)).astype(np.int32)


class Line:

    def __init__(self, engine, sem):
        self.e, self.sem, self.n, self.met = engine, sem, 0, {}

    def need(self, *marks):
        for sem, n in marks:
            if self.met.get(sem.name, 0) < n:
                self.e.wait_ge(sem, n)
                self.met[sem.name] = n

    def did(self, ins):
        self.n += 1
        ins.then_inc(self.sem, 1)
        return (self.sem, self.n)


class Arrival:

    def __init__(self, sem):
        self.sem, self.n = sem, 0

    def by(self, ins):
        self.n += 16
        ins.then_inc(self.sem, 16)
        return (self.sem, self.n)

    @property
    def all(self):
        return (self.sem, self.n)


class Slot:

    def __init__(self, ap, arrival=None):
        self.ap, self.freed, self.arrival = ap, (), arrival


class Ring:

    def __init__(self, slots):
        self.free = deque(slots)

    def has(self, n):
        return len(self.free) >= n

    def take(self):
        return self.free.popleft()

    def give(self, slot, *marks):
        slot.freed = marks
        self.free.append(slot)


class Lane:

    def __init__(self, works, depth, gap=1, young_first=False):
        self.step = -1 if young_first else 1
        self.works, self.depth, self.gap, self.since, self.active = deque(works), depth, gap, gap, []

    def turn(self):
        self.since += 1
        if self.works and len(self.active) < self.depth and self.since >= self.gap and self.works[0][0]():
            self.active.append(self.works.popleft()[1])
            self.since = 0
        going = [w for w in self.active[::self.step] if next(w, "done") != "done"]
        self.active = going[::self.step]
        return bool(self.works or self.active)


def emit(*lanes, until=None):
    for _ in range(20000):
        going = [lane.turn() for lane in lanes]
        if not any(going) or (until is not None and not (until.works or until.active)):
            return
    raise AssertionError("the lanes wait for each other")


def build(nc, t, out):
    const_np, at = constants()
    with ExitStack() as ctx:
        def sb(name, shape, dt=F32):
            return ctx.enter_context(nc.sbuf_tensor(name, shape, dt))

        def sem(name):
            return ctx.enter_context(nc.semaphore(name))

        pe = Line(nc.tensor, sem("pe_done"))
        dve = Line(nc.vector, sem("dve_done"))
        act = Line(nc.scalar, sem("act_done"))
        pool = Line(nc.gpsimd, sem("pool_done"))
        sp = Line(nc.sync, sem("sp_done"))
        sp_e, act_e, dve_e, pe_e, pool_e = sp.e, act.e, dve.e, pe.e, pool.e

        sent = nc.dram_tensor("sent", (DUMMY + NDUMMY * SLOTS, ROW), F32, kind="Internal").ap()
        padding = nc.dram_tensor("padding", (E * SLOTS, ROW), F32, kind="Internal").ap()
        back = nc.dram_tensor("back", (TRASH + NPAD * SLOTS, C), F32, kind="Internal").ap()

        X = sb("X", [P, NT, C])
        xT = sb("xT", [P, NT, P])
        consts = sb("consts", [P, const_np.shape[1]])
        addresses = sb("addresses", [P, K, NT], I32)
        w_attn0 = sb("w_attn0", [P, 4 * C])
        w_attn1 = sb("w_attn1", [P, 5 * C])
        w_shared = sb("w_shared", [P, 2 * FS + 3 * C])
        gates = sb("gates", [P, 2 * E])
        cols = sb("cols", [P, 5])
        bo1 = sb("bo1", [P, C])
        ones_bf = sb("ones_bf", [P, P], BF16)
        ones = sb("ones", [P, 1])
        before_bf = sb("before_bf", [P, P], BF16)
        bq0p1 = sb("bq0p1", [P, 1])
        pad_addresses = sb("pad_addresses", [P, NPAD, SUB], I32)

        def const(name):
            a, n = at[name]
            return consts[:, a:a + n]

        ident = const("ident")
        banks = [Slot(ctx.enter_context(nc.psum_tensor(f"bank{i}", [P, 512], F32))) for i in range(8)]
        psum = Ring(banks)

        def ring(name, n, shape, dt=F32, dma=False):
            return Ring([Slot(sb(f"{name}{i}", shape, dt), Arrival(sem(f"{name}{i}_dma")) if dma else None)
                         for i in range(n)])

        rows_ring = ring("rows", 2, [P, ST, K, ROW], dma=True)
        big = ring("big", 15, [P, 512])
        stage = ring("stage", 3, [P, max(W0COLS, W1COLS)], dma=True)
        v_heads = ring("v_heads", 3, [P, HEADS32, GT, C])

        brow_slot = stage.free[0]
        brow = brow_slot.ap[0:1, 0:4 * C]

        x_in = t["x"].rearrange("(n p) c -> p n c", p=P)
        x_arrival = [Arrival(sem(f"x{s}_dma")) for s in range(NS)]
        const_arrival = Arrival(sem("const_dma"))
        weight_arrival = Arrival(sem("weight_dma"))
        x_here = []

        def load_x(s):
            a = x_arrival[s]
            for h in range(2):
                j = ST * s + 8 * h
                a.by(sp_e.dma_start(X[:, j:j + 8, :], x_in[:, j:j + 8, :]))
            x_here.append(a.all)

        load_x(0)
        for dst, src in ((consts[:], t["consts"]), (addresses[:], t["addresses"]), (pad_addresses[:], t["pad_addresses"]), (gates[:], t["gates"]),
                         (cols[:], t["cols"]), (brow, t["brow"])):
            const_arrival.by(act_e.dma_start(dst, src))
        consts_here = const_arrival.all
        for dst, src in ((w_attn0[:], t["w_attn0"]), (w_attn1[:], t["w_attn1"]),
                         (w_shared[:], t["w_shared"]), (bo1[:], t["bo1"])):
            weight_arrival.by(act_e.dma_start(dst, src))
        weights_here = weight_arrival.all
        for s in range(1, NS):
            load_x(s)

        dve.did(dve_e.memset(ones_bf[:], 1.0))
        dve.did(dve_e.memset(ones[:], 1.0))
        dve.need(consts_here)
        dve.did(dve_e.tensor_copy(before_bf[:], const("before")))
        dve.did(dve_e.tensor_scalar(bq0p1[:], cols[:, 0:1], 1.0, None, ALU.add))
        F32R = mybir.dt.float32r
        brow_hi, brow_lo, ones_r = sb("brow_hi", [1, 4 * C], F32R), sb("brow_lo", [1, 4 * C], F32R), sb("ones_r", [1, P], F32R)
        m = dve.did(dve_e.tensor_copy(brow_hi[:], brow))
        dve.need(m)
        dve.did(dve_e.tensor_tensor(brow_lo[:], brow, brow_hi[:].bitcast(F32), ALU.subtract))
        brow_slot.freed = (dve.did(dve_e.tensor_scalar(ones_r[:], brow[:, 0:P], 0.0, 1.0, ALU.mult, ALU.add)),)
        dve.need(weights_here)
        wo1s = w_attn1[:, 4 * C:5 * C]
        made = dve.did(dve_e.tensor_scalar(wo1s, w_attn1[:, 4 * C:5 * C], cols[:, 3:4], 0.5, ALU.mult, ALU.mult))
        pe.need(consts_here, weights_here, made)
        act.need(consts_here, weights_here, made)
        pad_arrival = Arrival(sem("pad_dma"))
        pads_slot = rows_ring.free[-1]
        pads = pads_slot.ap[:].rearrange("p t k c -> p (t k) c")[:, 0:E * SUB, :].rearrange("p (n s) c -> p n s c", s=SUB)
        pool.need(pool.did(pool_e.memset(pads, 0.0)), consts_here)
        m = pool.did(pool_e.tensor_copy(pads[:, 0:NDUMMY, :, C].bitcast(I32), pad_addresses[:, E:NPAD, :]))
        sp.need(m)
        m = pad_arrival.by(sp_e.dma_start(sent[DUMMY:DUMMY + NDUMMY * SLOTS, :].rearrange("(n p) c -> p n c", p=P),
                                          pads[:, 0:NDUMMY, :, :].rearrange("p n s c -> p (n s) c")))
        pool.need(m)
        m = pool.did(pool_e.tensor_copy(pads[:, :, :, C].bitcast(I32), pad_addresses[:, 0:E, :]))
        sp.need(m)
        pads_kept = pad_arrival.by(sp_e.dma_start(padding.rearrange("(n p) c -> p n c", p=P), pads.rearrange("p n s c -> p (n s) c")))
        pads_slot.freed = (pads_kept,)

        stats = sb("stats", [P, ST, 6])
        moments = sb("moments", [P, ST, 2])
        rstd = sb("rstd", [P, ST])
        newton = sb("newton", [P, 3, ST])
        R8 = [sb(f"route{i}", [P, ST, E]) for i in range(7)]
        choice_bf = sb("choice_bf", [P, ST, E], BF16)
        R1 = [sb(f"gatev{i}", [P, ST]) for i in range(10)]
        slot_i = [sb(f"slot{k}", [P, 2, ST], I32) for k in range(K)]
        scan = [sb(f"scan{i}", [P, 8 + ST, E]) for i in range(2)]
        base = [sb(f"base{i}", [P, E]) for i in range(2)]
        counts_8 = sb("counts_8", [1, 6, 8 + E])
        counts_i = sb("counts_i", [1, 2, E], I32)
        table_i = [sb(f"table_i{n}", [1, 2, NTILES], I32) for n in range(2)]
        starts_i = [sb(f"starts_i{n}", [1, E], I32) for n in range(2)]
        half_bu = sb("half_bu", [P, 1])
        dve.did(dve_e.tensor_scalar(half_bu[:], cols[:, 4:5], 0.5, None, ALU.mult))
        for slot in v_heads.free:
            slot.freed = (pool.did(pool_e.memset(slot.ap[:], 0.0)),)
        for i in range(2):
            scans_zero = dve.did(dve_e.memset(scan[i][:], 0.0))
        counts_zero = dve.did(dve_e.memset(counts_8[:], 0.0))
        dve.need(scans_zero, counts_zero)

        def inverse_root(out, v, add, scratch, v_ready, state):
            a, y, z = (scratch[:, i, :] for i in range(3))
            dve.need(v_ready)
            m = dve.did(dve_e.tensor_scalar(a, v, add, None, ALU.add))
            dve.need(m)
            m = dve.did(dve_e.tensor_scalar(z.bitcast(I32), a.bitcast(I32), 1, None, ALU.logical_shift_right))
            dve.need(m)
            m = dve.did(dve_e.tensor_scalar(y.bitcast(I32), z.bitcast(I32), -1.0, float(0x5F3759DF), ALU.mult, ALU.add))
            for i in range(4):
                if i % 2:
                    yield
                dve.need(m)
                m = dve.did(dve_e.tensor_tensor(z, y, y, ALU.mult))
                dve.need(m)
                m = dve.did(dve_e.scalar_tensor_tensor(z, z, -0.5, a, ALU.mult, ALU.mult))
                dve.need(m)
                m = dve.did(dve_e.scalar_tensor_tensor(out if i == 3 else y, z, 1.5, y, ALU.add, ALU.mult))
            state["root"] = m

        def normalise(layer, s, state):
            while not rows_ring.has(1):
                yield
            rows = state["rows"][s] = rows_ring.take()
            dve.need(*rows.freed)
            act.need(*rows.freed)
            chunks = [(a, a + GT) for a in range(0, ST, GT)] if s == 0 else [(0, ST)]
            for c0, c1 in chunks:
                for j in range(c0, c1):
                    g = s * gps + j // GT
                    while g not in state["X_done"]:
                        yield
                    dve.need(state["X_done"][g])
                    m = dve.did(dve_e.bn_stats(stats[:, j, :], X[:, ST * s + j, :]))
                    if j % GT == GT - 1:
                        dve.need(m)
                        for i in range(j - GT + 1, j + 1):
                            m = dve.did(dve_e.bn_aggr(moments[:, i, :], stats[:, i, :]))
                        yield
                yield from inverse_root(rstd[:, c0:c1], moments[:, c0:c1, 1], LN_EPS, newton[:, :, c0:c1], m, state)
                dve.need(state["root"])
                for q in range(c0 // GT, c1 // GT):
                    g = s * gps + q
                    a, b = GT * q, GT * q + GT
                    for j in range(a, b):
                        m = dve.did(dve_e.tensor_scalar(rows.ap[:, j, 0, 0:C], X[:, ST * s + j, :], moments[:, j, 0:1],
                                                        rstd[:, j:j + 1], ALU.subtract, ALU.mult))
                    rows_ready = m
                    act.need(rows_ready)
                    state["copied"][s] = act.did(act_e.activation(rows.ap[:, a:b, 1, 0:C], rows.ap[:, a:b, 0, 0:C], ACT.Copy))
                    yield
                    while not psum.has(1):
                        yield
                    bank = psum.take()
                    pe.need(rows_ready, *bank.freed)
                    for j in range(a, b):
                        m = pe_e.transpose(bank.ap[:, (j - a) * P:(j - a + 1) * P], rows.ap[:, j, 0, 0:C], ident)
                    m = pe.did(m)
                    state["rows_read"][g] = rows_ready
                    yield
                    while layer == 1 and g not in state["xT_free"]:
                        yield
                    act.need(m, *state["xT_free"].get(g, ()))
                    m = act.did(act_e.activation(xT[:, GT * g:GT * g + GT, :].rearrange("p a b -> p (a b)"),
                                                 bank.ap[:], ACT.Copy))
                    psum.give(bank, m)
                    state["xT_ready"][g] = m
                    yield

        def route(layer, s, state):
            rows = state["rows"][s]
            while not psum.has(1):
                yield
            logits = psum.take()
            pe.need(*logits.freed, *(state["xT_ready"][s * gps + q] for q in range(gps)))
            for j in range(ST):
                m = pe_e.matmul(logits.ap[:, j * E:(j + 1) * E], xT[:, ST * s + j, :],
                                gates[:, layer * E:(layer + 1) * E], start=True, stop=True)
            m = pe.did(m)
            yield
            L = logits.ap[:, 0:ST * E].rearrange("p (a b) -> p a b", b=E)
            score, m1, m2, less, tmp, place, tmp2 = (r[:] for r in R8)

            def over_e(a):
                return a.unsqueeze(2).to_broadcast([P, ST, E])

            def over_j(a):
                return a.unsqueeze(1).to_broadcast([P, ST, E])

            best, second, z, p1, p2, den, w1, w2, e2, sl = (r[:] for r in R1)

            def v(ins):
                m = dve.did(ins)
                dve.need(m)
                return m

            dve.need(m)
            v(dve_e.tensor_reduce(best, L, AX, ALU.max))
            v(dve_e.tensor_tensor(tmp, L, over_e(best), ALU.is_equal))
            v(dve_e.tensor_tensor(tmp, tmp, over_j(const("first")), ALU.mult))
            v(dve_e.tensor_reduce(second, tmp, AX, ALU.max))
            yield
            v(dve_e.tensor_tensor(m1, tmp, over_e(second), ALU.is_equal))
            v(dve_e.scalar_tensor_tensor(less, m1, -BIG, L, ALU.mult, ALU.add))
            v(dve_e.tensor_reduce(second, less, AX, ALU.max))
            yield
            v(dve_e.tensor_tensor(tmp, less, over_e(second), ALU.is_equal))
            v(dve_e.tensor_tensor(tmp, tmp, over_j(const("first")), ALU.mult))
            v(dve_e.tensor_reduce(e2, tmp, AX, ALU.max))
            v(dve_e.tensor_tensor(m2, tmp, over_e(e2), ALU.is_equal))
            yield
            chosen = v(dve_e.tensor_tensor(choice_bf[:], m1, m2, ALU.add))
            shifted = v(dve_e.tensor_tensor(score, L, over_e(best), ALU.subtract))
            psum.give(logits, shifted)
            act.need(shifted)
            exps = act.did(act_e.activation(score, score, ACT.Exp))
            yield
            while not psum.has(1):
                yield
            ranks = psum.take()
            pe.need(chosen, *ranks.freed)
            flat = choice_bf[:].rearrange("p a b -> p (a b)")
            pe_e.matmul(ranks.ap[:, 0:ST * E], before_bf[:], flat, start=True, stop=True)
            m = pe.did(pe_e.matmul(ranks.ap[:, ST * E:2 * ST * E], ones_bf[:], flat, start=True, stop=True))
            yield
            dve.need(m)
            v(dve_e.tensor_copy(scan[0][:, 8:, :], ranks.ap[:, ST * E:2 * ST * E].rearrange("p (a b) -> p a b", b=E)))
            for i, d in enumerate((1, 2, 4, 8)):
                a, b = scan[i % 2], scan[(i + 1) % 2]
                v(dve_e.tensor_tensor(b[:, 8:, :], a[:, 8:, :], a[:, 8 - d:8 + ST - d, :], ALU.add))
                if i % 2:
                    yield
            v(dve_e.tensor_tensor(place, ranks.ap[:, 0:ST * E].rearrange("p (a b) -> p a b", b=E),
                                  scan[0][:, 7:7 + ST, :], ALU.add))
            psum.give(ranks, (dve.sem, dve.n))
            old = const("regions") if s == 0 else base[s % 2][:]
            v(dve_e.tensor_tensor(place, place, over_j(old), ALU.add))
            v(dve_e.tensor_tensor(base[(s + 1) % 2][:], old, scan[0][:, 7 + ST, :], ALU.add))
            for k, mk in enumerate((m1, m2)):
                v(dve_e.tensor_tensor(tmp, place, mk, ALU.mult))
                v(dve_e.tensor_reduce(sl, tmp, AX, ALU.add))
                placed = v(dve_e.tensor_copy(slot_i[k][:, s % 2, :], sl))
                yield
            dve.need(exps)
            v(dve_e.tensor_reduce(z, score, AX, ALU.add))
            v(dve_e.reciprocal(p1, z))
            v(dve_e.tensor_tensor(tmp2, score, m2, ALU.mult))
            v(dve_e.tensor_reduce(e2, tmp2, AX, ALU.add))
            yield
            v(dve_e.tensor_tensor(p2, e2, p1, ALU.mult))
            v(dve_e.scalar_tensor_tensor(den, p1, GATE_EPS if layer == 0 else 0.0, p2, ALU.add, ALU.add))
            v(dve_e.reciprocal(sl, den))
            dve.did(dve_e.tensor_tensor(rows.ap[:, :, 0, C + 1], p1, sl, ALU.mult))
            dve.did(dve_e.tensor_tensor(rows.ap[:, :, 1, C + 1], p2, sl, ALU.mult))
            for k in range(K):
                filled = dve.did(dve_e.tensor_copy(rows.ap[:, :, k, C].bitcast(I32),
                                                   addresses[:, k, ST * s:ST * s + ST]))
            state["routed"][s] = (placed, filled, state["copied"][s])

        def send(layer, s, state):
            rows = state["rows"][s]
            pool.need(*state["routed"][s])
            for j in range(ST):
                for k in range(K):
                    m = rows.arrival.by(pool_e.indirect_dma_start(
                        out=sent, out_offset=bass.IndirectOffsetOnAxis(ap=slot_i[k][:, s % 2, j:j + 1], axis=0),
                        in_=rows.ap[:, j, k, :], in_offset=None))
                yield
            state["sent"][s % 2] = m
            rows_ring.give(rows, m)

        def plan(layer, state):
            last = base[NS % 2]
            scratch = stage.take()
            dve.need(*scratch.freed)
            table_8 = scratch.ap[0:1, 0:2 * NTILES * E].rearrange("p (a b c) -> p a b c", a=2, b=NTILES)
            table_f = scratch.ap[0:1, 2 * NTILES * E:(2 * E + 5) * NTILES].rearrange("p (a b) -> p a b", b=NTILES)

            def v(ins):
                m = dve.did(ins)
                dve.need(m)
                return m

            n, up, c0, c1, nt, _ = (counts_8[:, i, 8:] for i in range(6))
            v(dve_e.tensor_copy(starts_i[layer][:], last[0:1, :]))
            v(dve_e.tensor_tensor(n, last[0:1, :], const("regions")[0:1, :], ALU.subtract))
            v(dve_e.tensor_scalar(counts_i[:, 0, :], n, float(SLOTS - 1), None, ALU.add))
            v(dve_e.tensor_scalar(counts_i[:, 1, :], counts_i[:, 0, :], SLOTS.bit_length() - 1, None,
                                  ALU.logical_shift_right))
            v(dve_e.tensor_copy(nt, counts_i[:, 1, :]))
            v(dve_e.tensor_copy(c0, nt))
            for i, d in enumerate((1, 2, 4)):
                a, b = 2 + i % 2, 2 + (i + 1) % 2
                v(dve_e.tensor_tensor(counts_8[:, b, 8:], counts_8[:, a, 8:], counts_8[:, a, 8 - d:8 + E - d], ALU.add))
            ends = counts_8[:, 3, 8:]
            tiles = const("tiles")[0:1, :]
            past, mine = table_8[:, 0, :, :], table_8[:, 1, :, :]
            shape = [1, NTILES, E]
            v(dve_e.tensor_tensor(past, tiles.unsqueeze(2).to_broadcast(shape),
                                  ends.unsqueeze(1).to_broadcast(shape), ALU.is_ge))
            v(dve_e.tensor_tensor(mine, past, nt.unsqueeze(1).to_broadcast(shape), ALU.mult))
            f = [table_f[:, i, :] for i in range(5)]
            v(dve_e.tensor_reduce(f[0], past, AX, ALU.add))
            v(dve_e.tensor_reduce(f[1], mine, AX, ALU.add))
            v(dve_e.tensor_tensor(f[2], tiles, f[1], ALU.subtract))
            v(dve_e.tensor_scalar(f[3], f[0], float(REGION), None, ALU.mult))
            v(dve_e.scalar_tensor_tensor(f[4], f[2], float(SLOTS), f[3], ALU.mult, ALU.add))
            v(dve_e.tensor_copy(table_i[layer][:, 1, :], f[4]))
            m = v(dve_e.tensor_scalar(table_i[layer][:, 0, :], f[0], float(E - 1), None, ALU.min))
            stage.give(scratch, m)
            sp.need(m, pads_kept)
            for e in range(E):
                r = sp_e.value_load(starts_i[layer][0:1, e:e + 1], min_val=0, max_val=DUMMY - SLOTS)
                pad_arrival.by(sp_e.dma_start(sent[bass.ds(r, SLOTS), :].rearrange("(s p) c -> p s c", p=P),
                                              padding[e * SLOTS:(e + 1) * SLOTS, :].rearrange("(s p) c -> p s c", p=P)))
                yield

        def add_bias(o, a, b):
            pe_e.matmul(o, ones_r[:], brow_hi[:, a:b], start=False, stop=False)
            return pe_e.matmul(o, ones_r[:], brow_lo[:, a:b], start=False, stop=True)

        def attention0(g, state):
            xg = xT[:, GT * g:GT * g + GT, :]
            pe.need(state["xT_ready"][g])
            while not psum.has(3):
                yield
            q_ps = psum.take()
            pe.need(*q_ps.freed)
            m_q = pe.did(pe_e.matmul(q_ps.ap[:], w_attn0[:, 0:C], xg.rearrange("p a b -> p (a b)"), start=True, stop=True))
            kv_ps, m_kv = [], []
            for h in range(2):
                bank = psum.take()
                pe.need(*bank.freed)
                for i in range(2):
                    o = bank.ap[:, 2 * C * i:2 * C * (i + 1)]
                    pe_e.matmul(o, xg[:, 2 * h + i, :], w_attn0[:, C:3 * C], start=True, stop=False)
                    m = add_bias(o, 0, 2 * C)
                kv_ps.append(bank)
                m_kv.append(pe.did(m))
            yield
            while not big.has(5):
                yield
            q, q_e = big.take(), big.take()
            act.need(m_q, *q_e.freed)
            m = act.did(act_e.activation(q_e.ap[:], q_ps.ap[:], ACT.Exp, bias=cols[:, 0:1]))
            dve.need(m)
            m = dve.did(dve_e.tensor_scalar(q_e.ap[:], q_e.ap[:], 1.0, None, ALU.min))
            dve.need(m, *q.freed)
            q_ready = dve.did(dve_e.scalar_tensor_tensor(q.ap[:], q_ps.ap[:], bq0p1[:], q_e.ap[:], ALU.add, ALU.max))
            psum.give(q_ps, q_ready)
            big.give(q_e, q_ready)
            k, k_e, v = big.take(), big.take(), big.take()
            k_ready, v_ready = [], []
            for h in range(2):
                src = kv_ps[h].ap[:].rearrange("p (a b) -> p a b", b=2 * C)
                c0, c1 = 2 * C * h, 2 * C * (h + 1)

                def half(s):
                    return s.ap[:, c0:c1].rearrange("p (a b) -> p a b", b=C)

                act.need(m_kv[h], *k_e.freed)
                m = act.did(act_e.activation(half(k_e), src[:, :, 0:C], ACT.Exp))
                act.need(*v.freed)
                v_ready.append(act.did(act_e.activation(half(v), src[:, :, C:2 * C], ACT.Copy)))
                dve.need(m)
                m = dve.did(dve_e.tensor_scalar(half(k_e), half(k_e), 1.0, None, ALU.min))
                dve.need(m, v_ready[h], *k.freed)
                k_ready.append(dve.did(dve_e.scalar_tensor_tensor(half(k), src[:, :, 0:C], 1.0, half(k_e), ALU.add, ALU.max)))
                psum.give(kv_ps[h], k_ready[h])
            big.give(k_e, *k_ready)
            yield
            while not psum.has(1):
                yield
            kv_bank = psum.take()
            pe.need(*kv_bank.freed)
            for h in range(2):
                pe.need(k_ready[h], v_ready[h])
                for i in range(2):
                    sl = slice((2 * h + i) * C, (2 * h + i + 1) * C)
                    m = pe_e.matmul(kv_bank.ap[:, h * P:(h + 1) * P], v.ap[:, sl], k.ap[:, sl], start=(i == 0), stop=(i == 1))
            m = pe.did(m)
            big.give(k, m)
            big.give(v, m)
            while not big.has(1):
                yield
            kvT = big.take()
            dve.need(m, *kvT.freed)
            m = dve.did(dve_e.tensor_tensor(kvT.ap[:, 0:2 * P].rearrange("p (a b) -> p a b", b=P),
                                            kv_bank.ap[:, 0:2 * P].rearrange("p (a b) -> p a b", b=P),
                                            const("heads0").unsqueeze(1).to_broadcast([P, 2, P]), ALU.mult))
            psum.give(kv_bank, m)
            yield
            while not psum.has(1):
                yield
            mix_bank = psum.take()
            pe.need(m, *mix_bank.freed)
            for h in range(2):
                m = pe_e.matmul(mix_bank.ap[:, h * C:(h + 1) * C], kvT.ap[:, h * P:(h + 1) * P], w_attn0[:, 3 * C:4 * C],
                                start=True, stop=True)
            m = pe.did(m)
            big.give(kvT, m)
            while not big.has(1):
                yield
            mix = big.take()
            act.need(m, *mix.freed)
            m = act.did(act_e.activation(mix.ap[:, 0:2 * C], mix_bank.ap[:, 0:2 * C], ACT.Copy))
            psum.give(mix_bank, m)
            yield
            while not psum.has(1):
                yield
            y = psum.take()
            pe.need(q_ready, m, *y.freed)
            for i in range(GT):
                o = y.ap[:, i * C:(i + 1) * C]
                pe_e.matmul(o, q.ap[:, i * P:(i + 1) * P], mix.ap[:, (i // 2) * C:(i // 2 + 1) * C], start=True, stop=False)
                m = add_bias(o, 2 * C, 3 * C)
            m = pe.did(m)
            big.give(q, m)
            big.give(mix, m)
            xr = X[:, GT * g:GT * g + GT, :].rearrange("p a b -> p (a b)")
            dve.need(m, state["rows_read"][g])
            m = dve.did(dve_e.tensor_tensor(xr, xr, y.ap[:], ALU.add))
            psum.give(y, m)
            state["X_after"][g] = m

        def shared(g, state):
            xg = xT[:, GT * g:GT * g + GT, :].rearrange("p a b -> p (a b)")
            pe.need(state["xT_ready"][g])
            h = []
            for c0, n in FSC:
                while not (psum.has(2) and big.has(2)):
                    yield
                gate, up = psum.take(), psum.take()
                pe.need(*gate.freed)
                m_g = pe.did(pe_e.matmul(gate.ap[0:n, :], w_shared[:, c0:c0 + n], xg, start=True, stop=True))
                pe.need(*up.freed)
                m_u = pe.did(pe_e.matmul(up.ap[0:n, :], w_shared[:, FS + c0:FS + c0 + n], xg, start=True, stop=True))
                s, hc = big.take(), big.take()
                act.need(m_g, *s.freed)
                m = act.did(act_e.activation(s.ap[0:n, :], gate.ap[0:n, :], ACT.Silu))
                psum.give(gate, m)
                dve.need(m, m_u, *hc.freed)
                m = dve.did(dve_e.tensor_tensor(hc.ap[0:n, :], s.ap[0:n, :], up.ap[0:n, :], ALU.mult))
                psum.give(up, m)
                big.give(s, m)
                h.append((hc, m, n))
                yield
            state["xT_free"][g] = (m_u,)
            while not psum.has(1):
                yield
            y = psum.take()
            pe.need(*y.freed, *(m for _, m, _ in h))
            for i in range(GT):
                for c, (hc, _, n) in enumerate(h):
                    m = pe_e.matmul(y.ap[:, i * C:(i + 1) * C], hc.ap[0:n, i * P:(i + 1) * P],
                                    w_shared[0:n, 2 * FS + c * C:2 * FS + (c + 1) * C], start=(c == 0), stop=(c == 2))
            m = pe.did(m)
            for hc, _, _ in h:
                big.give(hc, m)
            xr = X[:, GT * g:GT * g + GT, :].rearrange("p a b -> p (a b)")
            dve.need(m, state["X_after"][g])
            m = dve.did(dve_e.tensor_tensor(xr, xr, y.ap[:], ALU.add))
            psum.give(y, m)
            state["X_last"][g] = m

        tile_in = ring("tile_in", 4, [P, SUB, ROW], dma=True)
        tile_out = ring("tile_out", 3, [P, SUB, C], dma=True)
        return_marks = {}

        def fetch(layer, n, state):
            while not (stage.has(1) and tile_in.has(1)):
                yield
            w, r = stage.take(), tile_in.take()
            if n == 0:
                sp.need(*state["sent"], pad_arrival.all)
            ncols = (W0COLS, W1COLS)[layer]
            e = sp_e.value_load(table_i[layer][0:1, 0, n:n + 1], min_val=0, max_val=E - 1)
            first = sp_e.value_load(table_i[layer][0:1, 1, n:n + 1], min_val=0, max_val=DUMMY + (NDUMMY - 1) * SLOTS)
            sp.need(*r.freed)
            r_here = r.arrival.by(sp_e.dma_start(
                r.ap[:], sent[bass.ds(first, SLOTS), :].rearrange("(s p) c -> p s c", p=P)))
            sp.need(*w.freed)
            w_here = w.arrival.by(sp_e.dma_start(
                w.ap[:, 0:ncols], t[f"experts{layer}"][bass.ds(e, 1), :, :].rearrange("a p n -> p (a n)")))
            state["fetched"][n] = (w, r, w_here, r_here)

        def expert_tile(layer, n, state):
            w, r, w_here, r_here = state["fetched"][n]
            while not (psum.has(1) and big.has(1)):
                yield
            bank = psum.take()
            pe.need(r_here, *bank.freed)
            for i in range(SUB):
                m = pe_e.transpose(bank.ap[:, i * P:(i + 1) * P], r.ap[:, i, 0:C], ident)
            m = pe.did(m)
            x = big.take()
            x_eng = (dve, act)[layer == 0]
            x_eng.need(m, *x.freed)
            if layer == 0:
                x_ready = act.did(act_e.activation(x.ap[:], bank.ap[:], ACT.Copy))
            else:
                x_ready = dve.did(dve_e.tensor_copy(x.ap[:], bank.ap[:]))
            psum.give(bank, x_ready)
            yield
            yield
            pe.need(w_here, x_ready)
            h = []
            if layer == 0:
                while not (psum.has(3) and big.has(4)):
                    yield
                gate, up, tail = psum.take(), psum.take(), psum.take()
                pe.need(*gate.freed)
                m_g = pe.did(pe_e.matmul(gate.ap[:], w.ap[:, 0:P], x.ap[:], start=True, stop=True))
                pe.need(*up.freed)
                m_u = pe.did(pe_e.matmul(up.ap[:], w.ap[:, F0P + 64:2 * F0P], x.ap[:], start=True, stop=True))
                pe.need(*tail.freed)
                m_t = pe.did(pe_e.matmul(tail.ap[:], w.ap[:, P:2 * P], x.ap[:], start=True, stop=True))
                big.give(x, m_t)
                for n_h, src_g, src_u, m1, m2, slots in ((P, gate.ap, up.ap, m_g, m_u, (gate, up)),
                                                         (F0T, tail.ap, tail.ap[64:64 + F0T, :], m_t, m_t, (tail,))):
                    s, hc = big.take(), big.take()
                    act.need(m1, *s.freed)
                    m = act.did(act_e.activation(s.ap[0:n_h, :], src_g[0:n_h, :], ACT.Silu))
                    dve.need(m, m2, *hc.freed)
                    m = dve.did(dve_e.tensor_tensor(hc.ap[0:n_h, :], s.ap[0:n_h, :], src_u[0:n_h, :], ALU.mult))
                    for slot in slots:
                        psum.give(slot, m)
                    big.give(s, m)
                    h.append((hc, m, n_h))
                down, b1, b2 = 2 * F0P, None, None
            else:
                b1 = F1 + NC1 * C
                b2 = b1 + NC1
                down = F1
                for c in range(NC1):
                    while not (psum.has(1) and big.has(1)):
                        yield
                    z = psum.take()
                    pe.need(*z.freed)
                    m = pe.did(pe_e.matmul(z.ap[:], w.ap[:, c * P:(c + 1) * P], x.ap[:], start=True, stop=True))
                    hc = big.take()
                    act.need(m, w_here, *hc.freed)
                    m1 = act.did(act_e.activation(hc.ap[:], z.ap[:], ACT.Gelu, bias=w.ap[:, b1 + c:b1 + c + 1]))
                    psum.give(z, m1)
                    h.append((hc, m1, P))
                    if c % 2 == 1 and c < NC1 - 1:
                        yield
                big.give(x, m)
            yield
            yield
            while not (psum.has(1) and tile_out.has(1)):
                yield
            y = psum.take()
            pe.need(*y.freed, *(m for _, m, _ in h))
            for i in range(SUB):
                for c, (hc, _, k) in enumerate(h):
                    m = pe_e.matmul(y.ap[:, i * C:(i + 1) * C], hc.ap[0:k, i * P:(i + 1) * P],
                                    w.ap[0:k, down + c * C:down + (c + 1) * C], start=(c == 0), stop=(c == len(h) - 1))
            m_y = pe.did(m)
            for hc, _, _ in h:
                big.give(hc, m_y)
            o = tile_out.take()
            src = y.ap[:].rearrange("p (a b) -> p a b", b=C)
            dve.need(m_y, r_here, *o.freed)
            if layer == 1:
                dve.need(w_here)
                m = dve.did(dve_e.tensor_tensor(o.ap[:], src, w.ap[:, b2:b2 + C].unsqueeze(1).to_broadcast([P, SUB, C]), ALU.add))
                dve.need(m)
                psum.give(y, m)
                src = o.ap[:]
            m = dve.did(dve_e.tensor_tensor(o.ap[:], src, r.ap[:, :, C + 1:C + 2].to_broadcast([P, SUB, C]), ALU.mult))
            if layer == 0:
                psum.give(y, m)
            stage.give(w, m_y, m)
            yield
            pool.need(m)
            for i in range(SUB):
                m = o.arrival.by(pool_e.indirect_dma_start(
                    out=back, out_offset=bass.IndirectOffsetOnAxis(ap=r.ap[:, i, C:C + 1].bitcast(I32), axis=0),
                    in_=o.ap[:, i, :], in_offset=None))
            tile_out.give(o, m)
            tile_in.give(r, m)
            return_marks[o.arrival.sem.name] = m

        def collect(g, state):
            while not joined.has(K):
                yield
            sp.need(*return_marks.values())
            parts = []
            for k in range(K):
                part = joined.take()
                sp.need(*part.freed)
                rows = slice(k * TOK + g * GT * P, k * TOK + (g + 1) * GT * P)
                parts.append((part, part.arrival.by(sp_e.dma_start(
                    part.ap[:], back[rows, :].rearrange("(s p) c -> p s c", p=P)))))
            yield
            xr = X[:, GT * g:GT * g + GT, :]
            for part, here in parts:
                while g not in state["X_before"]:
                    yield
                dve.need(here, state["X_before"][g])
                m = dve.did(dve_e.tensor_tensor(xr, xr, part.ap[:], ALU.add))
                joined.give(part, m)
                state["X_before"][g] = m
            state["X_done"][g] = m

        joined = ring("joined", 4, [P, GT, C], dma=True)

        def attention1(g, state):
            xg = xT[:, GT * g:GT * g + GT, :]
            flat = xg.rearrange("p a b -> p (a b)")
            ready, mine = [], {}
            while not (big.has(HEADS64 + 5) and v_heads.has(1) and psum.has(4)):
                yield
            q, k, kh = big.take(), big.take(), [big.take() for _ in range(HEADS64)]
            v = v_heads.take()
            pe.need(state["xT_ready"][g])
            for c, dst in ((0, q), (1, k)):
                bank, e = psum.take(), big.take()
                pe.need(*bank.freed)
                m = pe.did(pe_e.matmul(bank.ap[:], w_attn1[:, c * C:(c + 1) * C], flat, start=True, stop=True))
                act.need(m, *e.freed)
                m = act.did(act_e.activation(e.ap[:], bank.ap[:], ACT.Exp, bias=cols[:, 1 + c:2 + c]))
                dve.need(m)
                m = dve.did(dve_e.tensor_scalar(e.ap[:], e.ap[:], 1.0, -1.0, ALU.min, ALU.add))
                dve.need(m, *dst.freed)
                m = dve.did(dve_e.scalar_tensor_tensor(dst.ap[:], bank.ap[:], cols[:, 1 + c:2 + c], e.ap[:], ALU.add, ALU.max))
                psum.give(bank, m)
                big.give(e, m)
                ready.append(m)
                yield
            q_ready, k_ready = ready
            while not (psum.has(1) and big.has(1)):
                yield
            bank, th = psum.take(), big.take()
            pe.need(*bank.freed)
            for i in range(GT):
                o = bank.ap[:, C * i:C * (i + 1)]
                pe_e.matmul(o, xg[:, i, :], w_attn1[:, 2 * C:3 * C], start=True, stop=False)
                m = add_bias(o, 3 * C, 4 * C)
            m = pe.did(m)
            act.need(m, *th.freed)
            m = act.did(act_e.activation(th.ap[:], bank.ap[:], ACT.Tanh, scale=0.5))
            dve.need(m, *v.freed)
            for s in range(HEADS32):
                dst, t_s, z_s = (a.rearrange("p (n s d) -> p n s d", s=HEADS32, d=D1)[:, :, s, :]
                                 for a in (v.ap[:, s, :, :].rearrange("p i c -> p (i c)"), th.ap[:], bank.ap[:]))
                m = dve.did(dve_e.scalar_tensor_tensor(dst, t_s, 1.0, z_s, ALU.add, ALU.mult))
            psum.give(bank, m)
            big.give(th, m)
            v_ready = m
            kh_ready = []
            for s in range(HEADS64):
                own = const("head_of_64")[:, s:s + 1]
                if s % 2:
                    act.need(k_ready, *kh[s].freed)
                    kh_ready.append(act.did(act_e.activation(kh[s].ap[:], k.ap[:], ACT.Copy, scale=own)))
                else:
                    dve.need(k_ready, *kh[s].freed)
                    kh_ready.append(dve.did(dve_e.tensor_scalar(kh[s].ap[:], k.ap[:], own, None, ALU.mult)))
            yield
            while not (psum.has(1) and big.has(2)):
                yield
            bank, th, u = psum.take(), big.take(), big.take()
            pe.need(*bank.freed)
            m = pe.did(pe_e.matmul(bank.ap[:], w_attn1[:, 3 * C:4 * C], flat, start=True, stop=True))
            act.need(m, *th.freed, *u.freed)
            act.did(act_e.activation(th.ap[:], bank.ap[:], ACT.Tanh, bias=half_bu[:], scale=0.5))
            m = act.did(act_e.activation(u.ap[:], bank.ap[:], ACT.Identity, bias=cols[:, 4:5]))
            psum.give(bank, m)
            dve.need(m)
            u_ready = dve.did(dve_e.scalar_tensor_tensor(u.ap[:], th.ap[:], 1.0, u.ap[:], ALU.add, ALU.mult))
            big.give(th, u_ready)
            yield
            while not (psum.has(1) and small2.has(1)):
                yield
            bank = psum.take()
            pe.need(k_ready, *bank.freed)
            for h in range(2):
                m = pe_e.transpose(bank.ap[:, h * P:(h + 1) * P], k.ap[:, 2 * h * P:(2 * h + 1) * P], ident)
            m = pe.did(m)
            k_tok = small2.take()
            act.need(m, *k_tok.freed)
            k_tok_ready = act.did(act_e.activation(k_tok.ap[:], bank.ap[:, 0:2 * P], ACT.Copy))
            psum.give(bank, k_tok_ready)
            big.give(k, m)
            yield
            while not (psum.has(1) and small2.has(1)):
                yield
            kv_bank = psum.take()
            pe.need(k_tok_ready, v_ready, *kv_bank.freed)
            for h in range(2):
                for s in range(HEADS32):
                    m = pe_e.matmul(kv_bank.ap[:, h * P:(h + 1) * P], k_tok.ap[:, h * P:(h + 1) * P], v.ap[:, s, 2 * h, :],
                                    start=(s == 0), stop=(s == HEADS32 - 1))
            m = pe.did(m)
            small2.give(k_tok, m)
            kv = small2.take()
            dve.need(m, *kv.freed)
            kv_ready = dve.did(dve_e.tensor_tensor(kv.ap[:].rearrange("p (a b) -> p a b", b=P),
                                                   kv_bank.ap[:, 0:2 * P].rearrange("p (a b) -> p a b", b=P),
                                                   const("heads1").unsqueeze(1).to_broadcast([P, 2, P]), ALU.mult))
            psum.give(kv_bank, kv_ready)
            yield
            while not (psum.has(3) and big.has(2)):
                yield
            att_bank = psum.take()

            def energies(h, j):
                bank, energy = psum.take(), big.take()
                rows64 = slice(64 * (j // 2), 64 * (j // 2) + 64)
                pe.need(q_ready, *kh_ready, *bank.freed)
                for i in range(2):
                    for s in range(HEADS32):
                        tok = slice((2 * h + i) * P, (2 * h + i + 1) * P)
                        m = pe_e.matmul(bank.ap[:, (2 * i + s) * P:(2 * i + s + 1) * P],
                                        kh[HEADS32 * (j % 2) + s].ap[rows64, tok], q.ap[rows64, tok],
                                        start=True, stop=True)
                m = pe.did(m)
                if j % 2:
                    dve.need(m, *energy.freed)
                    m = dve.did(dve_e.tensor_tensor(energy.ap[:].rearrange("p (a b) -> p a b", b=P),
                                                    bank.ap[:].rearrange("p (a b) -> p a b", b=P),
                                                    const("causal").unsqueeze(1).to_broadcast([P, 4, P]), ALU.mult))
                    psum.give(bank, m)
                else:
                    act.need(m, *energy.freed)
                    m = act.did(act_e.activation(energy.ap[:], bank.ap[:], ACT.Copy, scale=0.5))
                    psum.give(bank, m)
                    pool.need(m)
                    blocks = energy.ap[:].rearrange("p (a b) -> p a b", b=P)
                    m = pool.did(pool_e.affine_select(out=blocks, in_=blocks, pattern=[[0, 4], [1, P]], compare_op=ALU.is_ge,
                                                      fill=0.0, base=0, channel_multiplier=-1))
                return energy, m

            def gather(h, j, energy, masked):
                pe.need(masked)
                for i in range(2):
                    for s in range(HEADS32):
                        tile = 2 * h + i
                        m = pe_e.matmul(att_bank.ap[32 * j:32 * j + 32, tile * P:(tile + 1) * P],
                                        v.ap[:, s, tile, 32 * j:32 * j + 32], energy.ap[:, (2 * i + s) * P:(2 * i + s + 1) * P],
                                        start=False, stop=(h == 1 and i == 1 and s == HEADS32 - 1), skip_group_check=True)
                m = pe.did(m)
                big.give(energy, m)
                return m

            pending = []
            for h in range(2):
                for j in range(H1 // HEADS32):
                    while not (psum.has(1) and big.has(1)):
                        yield
                    pending.append((h, j, *energies(h, j)))
                    if h == 0 and j == 0:
                        pe.need(kv_ready, *att_bank.freed)
                        for b in range(2):
                            tile = 2 * b + 1
                            m = pe_e.matmul(att_bank.ap[:, tile * P:(tile + 1) * P], kv.ap[:, b * P:(b + 1) * P],
                                            q.ap[:, tile * P:(tile + 1) * P], start=(b == 0), stop=False, skip_group_check=True)
                        small2.give(kv, pe.did(m))
                    yield
                    if len(pending) > 2:
                        m = gather(*pending.pop(0))
            while pending:
                m = gather(*pending.pop(0))
            att_done = m
            big.give(q, m)
            for s in kh:
                big.give(s, m)
            v_heads.give(v, m)
            while not (big.has(2) and sums.has(1) and psum.has(1)):
                yield
            sq, uo, ss, bank = big.take(), big.take(), sums.take(), psum.take()
            dve.need(att_done, u_ready, *uo.freed)
            uo_ready = dve.did(dve_e.tensor_tensor(uo.ap[:], att_bank.ap[:], u.ap[:], ALU.mult))
            act.need(uo_ready, *sq.freed)
            m_sq = act.did(act_e.activation(sq.ap[:], att_bank.ap[:], ACT.Square))
            psum.give(att_bank, uo_ready, m_sq)
            big.give(u, uo_ready)
            yield
            pe.need(m_sq, *bank.freed)
            for i in range(GT):
                m = pe_e.matmul(bank.ap[:, i:i + 1], sq.ap[:, i * P:(i + 1) * P], ones[:], start=True, stop=True)
            m = pe.did(m)
            big.give(sq, m)
            tot = ss.ap[:, 3, :]
            dve.need(m, *ss.freed)
            m = dve.did(dve_e.tensor_copy(tot, bank.ap[:, 0:GT]))
            psum.give(bank, m)
            yield from inverse_root(ss.ap[:, 4, :], tot, 0.0, ss.ap[:, 0:3, :], m, mine)
            dve.need(mine["root"])
            m = dve.did(dve_e.tensor_tensor(ss.ap[:, 0, :], tot, ss.ap[:, 4, :], ALU.mult))
            dve.need(m)
            m = dve.did(dve_e.tensor_scalar(ss.ap[:, 1, :], ss.ap[:, 0, :], float(C) ** -0.5, RMS_EPS, ALU.mult, ALU.add))
            dve.need(m)
            inv_ready = dve.did(dve_e.reciprocal(ss.ap[:, 5, :], ss.ap[:, 1, :]))
            yield
            while not psum.has(1):
                yield
            y = psum.take()
            pe.need(uo_ready, *y.freed)
            for i in range(GT):
                m = pe_e.matmul(y.ap[:, i * C:(i + 1) * C], uo.ap[:, i * P:(i + 1) * P], wo1s, start=True, stop=True)
            m_y = pe.did(m)
            big.give(uo, m_y)
            xr = X[:, GT * g:GT * g + GT, :]
            dve.need(state["X_done"][g], state["rows_read"][g])
            m = dve.did(dve_e.tensor_tensor(xr, xr, bo1[:].unsqueeze(1).to_broadcast([P, GT, C]), ALU.add))
            dve.need(m, m_y, inv_ready)
            for i in range(GT):
                m = dve.did(dve_e.scalar_tensor_tensor(X[:, GT * g + i, :], y.ap[:, i * C:(i + 1) * C], ss.ap[:, 5, i:i + 1],
                                                       X[:, GT * g + i, :], ALU.mult, ALU.add))
            psum.give(y, m)
            sums.give(ss, m)
            state["X_after"][g] = m

        small2 = ring("small2", 5, [P, 2 * P])
        sums = ring("sums", 3, [P, 6, GT])

        loan_arrivals = {}

        def lend(src, dst, width, split=None, dma=None):
            loans = []
            while src.has(1):
                slot = src.take()
                whole = slot.ap[:]
                if len(whole.shape) > 2:
                    whole = whole.rearrange({3: "p a b -> p (a b)", 4: "p a b c -> p (a b c)"}[len(whole.shape)])
                parts = []
                for i in range(whole.shape[1] // width):
                    ap = whole[:, i * width:(i + 1) * width]
                    parts.append(Slot(ap.rearrange("p (s c) -> p s c", s=split) if split else ap))
                    if dma:
                        name = f"{dma}{len(loans)}_{i}_dma"
                        if name not in loan_arrivals:
                            loan_arrivals[name] = Arrival(sem(name))
                        parts[-1].arrival = loan_arrivals[name]
                    parts[-1].freed = slot.freed
                    dst.free.append(parts[-1])
                loans.append((slot, parts))
            return src, dst, loans

        def reclaim(src, dst, loans):
            for slot, parts in loans:
                for part in parts:
                    dst.free.remove(part)
                src.give(slot, *(m for part in parts for m in part.freed))

        def lend_to_attention():
            return [lend(r, big, 512) for r in (stage, tile_in, tile_out)]

        def lend_to_experts():
            kept = rows_ring.take()
            loans = [lend(rows_ring, stage, max(W0COLS, W1COLS), dma="lent_stage")]
            rows_ring.free.append(kept)
            loans.append(lend(rows_ring, tile_in, SUB * ROW, SUB, dma="lent_tile"))
            return loans

        def new_state(**kw):
            return {"rows": {}, "rows_read": {}, "copied": {}, "routed": {}, "xT_ready": {}, "xT_free": {}, "X_done": {},
                    "X_after": {}, "X_last": {}, "sent": [None, None], "fetched": {}} | kw

        def when(d, *keys):
            return lambda: all(x in d for x in keys)

        def always():
            return True

        def lanes_of(layer, L, attention, attention_depth):
            return [
                Lane([(when(L["xT_ready"], g), attention(g, L)) for g in range(NG)], attention_depth, 2),
                Lane([(always, normalise(layer, s, L)) for s in range(NS)], 1),
                Lane([(when(L["xT_ready"], *range(s * gps, (s + 1) * gps)), route(layer, s, L)) for s in range(NS)], 1),
                Lane([(when(L["routed"], s), send(layer, s, L)) for s in range(NS)], 1),
            ]

        def fetches(layer, L):
            return Lane([(always, fetch(layer, n, L)) for n in range(NTILES)], 1)

        def experts(layer, L, gap):
            return Lane([(when(L["fetched"], n), expert_tile(layer, n, L)) for n in range(NTILES)], 3, gap, young_first=True)

        L0 = new_state(X_done={g: x_here[g // gps] for g in range(NG)})
        loans = lend_to_attention()
        emit(*lanes_of(0, L0, attention0, 3))
        for loan in loans:
            reclaim(*loan)
        loans = lend_to_experts()
        late = 3
        planned = Lane([(always, plan(0, L0))], 1)
        early_shared = Lane([(always, shared(g, L0)) for g in range(3)], 1)
        emit(planned, early_shared, fetches_0 := fetches(0, L0), until=early_shared)
        emit(planned, fetches_0, experts(0, L0, 2), Lane([(always, shared(g, L0)) for g in range(3, NG - late)], 1, 12))

        for loan in loans[::-1]:
            reclaim(*loan)
        loans = lend_to_attention()
        L1 = new_state(xT_free=L0["xT_free"], X_before=L0["X_last"])
        emit(Lane([(always, shared(g, L0)) for g in range(NG - late, NG)], 1),
             Lane([(always, collect(g, L1)) for g in range(NG)], 2, 2),
             *lanes_of(1, L1, attention1, 3))
        for loan in loans:
            reclaim(*loan)
        loans = lend_to_experts()
        planned, fetches_1 = Lane([(always, plan(1, L1))], 1), fetches(1, L1)
        emit(planned, fetches_1, experts(1, L1, 3))

        out_arrival = Arrival(sem("out_dma"))
        y_out = out.rearrange("(n p) c -> p n c", p=P)
        L2 = new_state(X_before=L1["X_after"])

        def finish(g, state):
            yield from collect(g, state)
            act.need(state["X_done"][g])
            out_arrival.by(act_e.dma_start(y_out[:, GT * g:GT * g + GT, :], X[:, GT * g:GT * g + GT, :]))

        emit(Lane([(always, finish(g, L2)) for g in range(NG)], 2))
        act.need(out_arrival.all)


def kernel(**inputs):
    import concourse.bacc as bacc
    from concourse.bass_utils import run_bass_kernel_spmd

    i = {k: np.asarray(v) for k, v in inputs.items()}

    def padded(a, n):
        return np.concatenate([a, np.zeros((*a.shape[:-1], n - a.shape[-1]), a.dtype)], axis=-1)

    def padded_rows(a, n):
        return np.concatenate([a, np.zeros((*a.shape[:-2], n - a.shape[-2], a.shape[-1]), a.dtype)], axis=-2)

    wd = padded_rows(i["L0_ffn_wd"], 2 * P)
    wu = i["L0_ffn_wu"]
    experts0 = np.concatenate([padded(i["L0_ffn_wg"], F0P), padded(wu[:, :, P:], 64), wu[:, :, 0:P], wd[:, 0:P], wd[:, P:2 * P]], axis=2)
    w2 = i["L1_ffn_w2"].reshape(E, NC1, P, C).transpose(0, 2, 1, 3).reshape(E, P, NC1 * C)
    b1 = i["L1_ffn_b1"].reshape(E, NC1, P).transpose(0, 2, 1)
    b2 = np.broadcast_to(i["L1_ffn_b2"][:, None, :], (E, P, C))
    experts1 = np.concatenate([i["L1_ffn_w1"], w2, b1, b2], axis=2)
    swd = padded_rows(i["L0_ffn_swd"], 3 * P)
    arrays = {
        "x": i["L0_attn_x"].reshape(TOK, C),
        "consts": constants()[0],
        "addresses": return_addresses(),
        "pad_addresses": padding_addresses(),
        "gates": np.concatenate([i["L0_ffn_gate_w"].T, i["L1_ffn_w_router"].T], axis=1),
        "cols": np.stack([i["L0_attn_bq"], i["L1_attn_bq"], i["L1_attn_bk"], i["L1_attn_scale"], i["L1_attn_bu"]], axis=1),
        "brow": np.concatenate([i["L0_attn_bk"], i["L0_attn_bv"], i["L0_attn_bo"], i["L1_attn_bv"]])[None, :],
        "w_attn0": np.concatenate([i[f"L0_attn_W{n}"].T for n in "qkvo"], axis=1),
        "w_attn1": np.concatenate([i[f"L1_attn_W{n}"].T for n in "qkvuo"], axis=1),
        "w_shared": np.concatenate([i["L0_ffn_swg"], i["L0_ffn_swu"], swd[0:P], swd[P:2 * P], swd[2 * P:3 * P]], axis=1),
        "bo1": np.broadcast_to(i["L1_attn_bo"][None, :], (P, C)),
        "experts0": experts0,
        "experts1": experts1,
    }
    nc = bacc.Bacc("TRN2", target_bir_lowering=False, num_devices=1)
    feed, t = {}, {}
    for name, a in arrays.items():
        a = np.ascontiguousarray(a)
        feed[f"in_{name}"] = a
        t[name] = nc.dram_tensor(f"in_{name}", a.shape, mybir.dt.from_np(a.dtype), kind="ExternalInput").ap()
    out = nc.dram_tensor("out", (TOK, C), F32, kind="ExternalOutput").ap()
    build(nc, t, out)
    r = run_bass_kernel_spmd(nc, [feed], core_ids=[0])
    return r.results[0]["out"].reshape(B, S, C)
```

```python
from collections import deque
from contextlib import ExitStack

import concourse.bass as bass
import numpy as np
from concourse import mybir
from concourse.alu_op_type import AluOpType as ALU

F32 = mybir.dt.float32
I32 = mybir.dt.int32
BF16 = mybir.dt.bfloat16
F32R = mybir.dt.float32r
ACT = mybir.ActivationFunctionType
AX = mybir.AxisListType.X

P = 128
B, S, C = 32, 256, 128
TOK = B * S
NT = TOK // P
GT = 4
NG = NT // GT
ST = 16
NS = NT // ST
gps = ST // GT
E = 8
K = 2
SLOTS = 512
SUB = SLOTS // P
NTILES = (K * TOK - E) // SLOTS + E
REGION = TOK + SLOTS
DUMMY = E * REGION
NDUMMY = NTILES - K * TOK // SLOTS
ROW = C + 2
TRASH = K * TOK
NPAD = E + NDUMMY
H0, D0 = 16, 8
H1, D1 = 8, 16
HEADS32 = 32 // D1
HEADS64 = 64 // D1
F0 = 176
F0P = 192
F0T = F0 - P
FS = 352
FSC = [(0, 128), (128, 128), (256, 96)]
F1 = 512
NC1 = F1 // P
W0COLS = 2 * F0P + 2 * C
W1COLS = F1 + NC1 * C + NC1 + C
LN_EPS = 1e-5
RMS_EPS = 1e-8
GATE_EPS = 1e-20
BIG = 3.0e38


def constants():
    p = np.arange(P)
    blocks = {
        "ident": np.eye(P),
        "before": p[:, None] < p[None, :],
        "causal": 0.5 * (p[:, None] <= p[None, :]),
        "heads0": p[:, None] // D0 == p[None, :] // D0,
        "heads1": 0.5 * (p[:, None] // D1 == p[None, :] // D1),
        "head_of_64": (p[:, None] // D1) % HEADS64 == np.arange(HEADS64)[None, :],
        "first": np.broadcast_to(E - np.arange(E), (P, E)),
        "regions": np.broadcast_to(np.arange(E) * REGION, (P, E)),
        "tiles": np.broadcast_to(np.arange(NTILES), (P, NTILES)),
    }
    at, cols = {}, 0
    for name, block in blocks.items():
        at[name] = (cols, block.shape[1])
        cols += block.shape[1]
    return np.concatenate([b.astype(np.float32) for b in blocks.values()], axis=1), at


def return_addresses():
    token = np.arange(NT)[None, :] * P + np.arange(P)[:, None]
    return np.stack([token + k * TOK for k in range(K)], axis=1).astype(np.int32)


def padding_addresses():
    n = np.arange(NPAD * SUB).reshape(1, NPAD, SUB)
    return (TRASH + n * P + np.arange(P).reshape(P, 1, 1)).astype(np.int32)


def pause(name):
    for _ in range(PAUSES[name]):
        yield


class Line:

    def __init__(self, engine, sem):
        self.e, self.sem, self.n, self.met = engine, sem, 0, {}

    def need(self, *marks):
        for sem, n in marks:
            if self.met.get(sem.name, 0) < n:
                self.e.wait_ge(sem, n)
                self.met[sem.name] = n

    def did(self, ins):
        self.n += 1
        ins.then_inc(self.sem, 1)
        return (self.sem, self.n)


class Arrival:

    def __init__(self, sem):
        self.sem, self.n = sem, 0

    def by(self, ins):
        self.n += 16
        ins.then_inc(self.sem, 16)
        return (self.sem, self.n)

    @property
    def all(self):
        return (self.sem, self.n)


class Slot:

    def __init__(self, ap, arrival=None):
        self.ap, self.freed, self.arrival = ap, (), arrival


class Ring:

    def __init__(self, slots):
        self.free = deque(slots)

    def has(self, n):
        return len(self.free) >= n

    def take(self):
        return self.free.popleft()

    def give(self, slot, *marks):
        slot.freed = marks
        self.free.append(slot)


class Lane:

    def __init__(self, works, depth, gap=1, young_first=False):
        self.step = -1 if young_first else 1
        self.works, self.depth, self.gap, self.since, self.active = deque(works), depth, gap, gap, []

    def turn(self):
        self.since += 1
        if self.works and len(self.active) < self.depth and self.since >= self.gap and self.works[0][0]():
            self.active.append(self.works.popleft()[1])
            self.since = 0
        going = [w for w in self.active[::self.step] if next(w, "done") != "done"]
        self.active = going[::self.step]
        return bool(self.works or self.active)


def emit(*lanes, until=None):
    for _ in range(20000):
        going = [lane.turn() for lane in lanes]
        if not any(going) or (until is not None and not (until.works or until.active)):
            return
    raise AssertionError("the lanes wait for each other")


AHEAD = [5, 3]
LATE = 1
EARLY = 1
ATT0 = (4, 2)
ATT1 = (3, 6)
SHARED = (2, 4)
COLLECT = (1, 4)
PENDING = 3
PAUSES = {'rows': 3, 'rstd': 1, 'kv0': 2, 'mix0': 2, 'y0': 1, 'down': 1, 'qk1': 1, 'squares': 1, 'root': 1}
ORDER = [(2, 3, 0, 1), (0, 1, 2, 3)]


def build(nc, t, out):
    const_np, at = constants()
    with ExitStack() as ctx:
        def sb(name, shape, dt=F32):
            return ctx.enter_context(nc.sbuf_tensor(name, shape, dt))

        def sem(name):
            return ctx.enter_context(nc.semaphore(name))

        pe = Line(nc.tensor, sem("pe_done"))
        dve = Line(nc.vector, sem("dve_done"))
        act = Line(nc.scalar, sem("act_done"))
        pool = Line(nc.gpsimd, sem("pool_done"))
        sp = Line(nc.sync, sem("sp_done"))
        sp_e, act_e, dve_e, pe_e, pool_e = sp.e, act.e, dve.e, pe.e, pool.e

        sent = nc.dram_tensor("sent", (DUMMY + NDUMMY * SLOTS, ROW), F32, kind="Internal").ap()
        padding = nc.dram_tensor("padding", (E * SLOTS, ROW), F32, kind="Internal").ap()
        back = nc.dram_tensor("back", (TRASH + NPAD * SLOTS, C), F32, kind="Internal").ap()

        X = sb("X", [P, NT, C])
        xT = sb("xT", [P, NT, P])
        consts = sb("consts", [P, const_np.shape[1]])
        addresses = sb("addresses", [P, K, NT], I32)
        w_attn0 = sb("w_attn0", [P, 4 * C])
        w_attn1 = sb("w_attn1", [P, 5 * C])
        w_shared = sb("w_shared", [P, 2 * FS + 3 * C])
        gates = sb("gates", [P, 2 * E])
        cols = sb("cols", [P, 5])
        bo1 = sb("bo1", [P, C])
        ones_bf = sb("ones_bf", [P, P], BF16)
        ones = sb("ones", [P, 1])
        before_bf = sb("before_bf", [P, P], BF16)
        bq0p1 = sb("bq0p1", [P, 1])
        pad_addresses = sb("pad_addresses", [P, NPAD, SUB], I32)

        def const(name):
            a, n = at[name]
            return consts[:, a:a + n]

        ident = const("ident")
        banks = [Slot(ctx.enter_context(nc.psum_tensor(f"bank{i}", [P, 512], F32))) for i in range(8)]
        psum = Ring(banks)

        arrivals = {}

        def ring(name, n, shape, dt=F32, dma=False, scope=ctx):
            slots = []
            for i in range(n):
                slot = Slot(scope.enter_context(nc.sbuf_tensor(f"{name}{i}_{len(scopes)}", shape, dt)))
                if dma:
                    if f"{name}{i}" not in arrivals:
                        arrivals[f"{name}{i}"] = Arrival(sem(f"{name}{i}_dma"))
                    slot.arrival = arrivals[f"{name}{i}"]
                slots.append(slot)
            return Ring(slots)

        scopes = []
        rings = {}
        big = ring("big", 15, [P, 512])
        v_heads = ring("v_heads", 3, [P, HEADS32, GT, C])

        brow_slot = big.free[0]
        brow = brow_slot.ap[0:1, 0:4 * C]

        x_in = t["x"].rearrange("(n p) c -> p n c", p=P)
        x_arrival = [Arrival(sem(f"x{i}_dma")) for i in range(gps + NS - 1)]
        const_arrival = Arrival(sem("const_dma"))
        weight_arrival = Arrival(sem("weight_dma"))
        x_here = []

        def load_x(s):
            for g in range(gps * s, gps * (s + 1)):
                a = x_arrival[g if s == 0 else gps + s - 1]
                a.by(sp_e.dma_start(X[:, GT * g:GT * (g + 1), :], x_in[:, GT * g:GT * (g + 1), :]))
                x_here.append(a)

        load_x(0)
        for dst, src in ((consts[:], t["consts"]), (addresses[:], t["addresses"]), (pad_addresses[:], t["pad_addresses"]),
                         (gates[:], t["gates"]), (cols[:], t["cols"]), (brow, t["brow"])):
            const_arrival.by(act_e.dma_start(dst, src))
        consts_here = const_arrival.all
        for dst, src in ((w_attn0[:], t["w_attn0"]), (w_attn1[:], t["w_attn1"]),
                         (w_shared[:], t["w_shared"]), (bo1[:], t["bo1"])):
            weight_arrival.by(act_e.dma_start(dst, src))
        weights_here = weight_arrival.all
        sp.need(consts_here)
        load_x(1)
        sp.need(weights_here)
        for s in range(2, NS):
            load_x(s)

        dve.did(dve_e.memset(ones_bf[:], 1.0))
        dve.did(dve_e.memset(ones[:], 1.0))
        dve.need(consts_here)
        dve.did(dve_e.tensor_copy(before_bf[:], const("before")))
        dve.did(dve_e.tensor_scalar(bq0p1[:], cols[:, 0:1], 1.0, None, ALU.add))
        brow_hi, brow_lo = sb("brow_hi", [1, 4 * C], F32R), sb("brow_lo", [1, 4 * C], F32R)
        ones_r = sb("ones_r", [1, P], F32R)
        m = dve.did(dve_e.tensor_copy(brow_hi[:], brow))
        dve.need(m)
        dve.did(dve_e.tensor_tensor(brow_lo[:], brow, brow_hi[:].bitcast(F32), ALU.subtract))
        brow_slot.freed = (dve.did(dve_e.tensor_scalar(ones_r[:], brow[:, 0:P], 0.0, 1.0, ALU.mult, ALU.add)),)
        pe.need(consts_here)
        act.need(consts_here)
        pad_arrival = Arrival(sem("pad_dma"))
        pads_at = NT * P - E * SUB * ROW
        pads = xT[:].rearrange("p a b -> p (a b)")[:, pads_at:].rearrange("p (n s c) -> p n s c", n=E, s=SUB)
        pool.need(pool.did(pool_e.memset(pads, 0.0)), consts_here)
        m = pool.did(pool_e.tensor_copy(pads[:, 0:NDUMMY, :, C].bitcast(I32), pad_addresses[:, E:NPAD, :]))
        sp.need(m)
        m = pad_arrival.by(sp_e.dma_start(sent[DUMMY:DUMMY + NDUMMY * SLOTS, :].rearrange("(n p) c -> p n c", p=P),
                                          pads[:, 0:NDUMMY, :, :].rearrange("p n s c -> p (n s) c")))
        pool.need(m)
        m = pool.did(pool_e.tensor_copy(pads[:, :, :, C].bitcast(I32), pad_addresses[:, 0:E, :]))
        sp.need(m)
        pads_kept = pad_arrival.by(sp_e.dma_start(padding.rearrange("(n p) c -> p n c", p=P), pads.rearrange("p n s c -> p (n s) c")))

        stats = sb("stats", [P, ST, 6])
        moments = sb("moments", [P, ST, 2])
        rstd = sb("rstd", [P, ST])
        variance = sb("variance", [P, ST])
        exponents = {e: sb(f"exponents{i}", [P, ST]) for i, e in enumerate((-0.5, 0.5))}
        for e, ap in exponents.items():
            pool.need(pool.did(pool_e.memset(ap[:], e)))
        R8 = [sb(f"route{i}", [P, ST, E]) for i in range(7)]
        choice_bf = sb("choice_bf", [P, ST, E], BF16)
        R1 = [sb(f"gatev{i}", [P, ST]) for i in range(10)]
        slot_i = [sb(f"slot{k}", [P, 2, ST], I32) for k in range(K)]
        scan = [sb(f"scan{i}", [P, 8 + ST, E]) for i in range(2)]
        base = [sb(f"base{i}", [P, E]) for i in range(2)]
        counts_8 = sb("counts_8", [1, 6, 8 + E])
        counts_i = sb("counts_i", [1, 2, E], I32)
        table_i = [sb(f"table_i{n}", [1, 2, NTILES], I32) for n in range(2)]
        starts_i = [sb(f"starts_i{n}", [1, E], I32) for n in range(2)]
        half_bu = sb("half_bu", [P, 1])
        for slot in v_heads.free:
            slot.freed = (pool.did(pool_e.memset(slot.ap[:], 0.0)),)
        for i in range(2):
            scans_zero = dve.did(dve_e.memset(scan[i][:], 0.0))
        counts_zero = dve.did(dve_e.memset(counts_8[:], 0.0))
        dve.need(scans_zero, counts_zero)

        def power(out, v, exponent, v_ready):
            pool.need(*v_ready)
            return pool.did(pool_e.tensor_tensor(out, v, exponents[exponent][:, 0:v.shape[1]], ALU.pow))

        def normalise(layer, s, state):
            while not rings["rows"].has(1):
                yield
            rows = state["rows"][s] = rings["rows"].take()
            dve.need(*rows.freed)
            act.need(*rows.freed)
            chunks = [(a, a + GT) for a in range(0, ST, GT)] if s == 0 else [(0, ST)]
            for c0, c1 in chunks:
                for j in range(c0, c1):
                    g = s * gps + j // GT
                    while g not in state["X_done"]:
                        yield
                    dve.need(state["X_done"][g])
                    m = dve.did(dve_e.bn_stats(stats[:, j, :], X[:, ST * s + j, :]))
                    if j % GT == GT - 1:
                        dve.need(m)
                        for i in range(j - GT + 1, j + 1):
                            m = dve.did(dve_e.bn_aggr(moments[:, i, :], stats[:, i, :]))
                        yield
                dve.need(m)
                m = dve.did(dve_e.tensor_scalar(variance[:, c0:c1], moments[:, c0:c1, 1], LN_EPS, None, ALU.add))
                m = power(rstd[:, c0:c1], variance[:, c0:c1], -0.5, (m,))
                yield from pause("rstd")
                dve.need(m)
                for q in range(c0 // GT, c1 // GT):
                    g = s * gps + q
                    a, b = GT * q, GT * q + GT
                    for j in range(a, b):
                        m = dve.did(dve_e.tensor_scalar(rows.ap[:, j, 0, 0:C], X[:, ST * s + j, :], moments[:, j, 0:1],
                                                        rstd[:, j:j + 1], ALU.subtract, ALU.mult))
                    rows_ready = m
                    act.need(rows_ready)
                    state["copied"][s] = act.did(act_e.activation(rows.ap[:, a:b, 1, 0:C], rows.ap[:, a:b, 0, 0:C], ACT.Copy))
                    yield from pause("rows")
                    while not psum.has(1):
                        yield
                    bank = psum.take()
                    pe.need(rows_ready, *bank.freed)
                    for j in range(a, b):
                        m = pe_e.transpose(bank.ap[:, (j - a) * P:(j - a + 1) * P], rows.ap[:, j, 0, 0:C], ident)
                    m = pe.did(m)
                    state["rows_read"][g] = rows_ready
                    yield
                    while layer == 1 and g not in state["xT_free"]:
                        yield
                    act.need(m, *state["xT_free"].get(g, ()))
                    if (g + 1) * GT * P > pads_at:
                        act.need(pads_kept)
                    m = act.did(act_e.activation(xT[:, GT * g:GT * g + GT, :].rearrange("p a b -> p (a b)"),
                                                 bank.ap[:], ACT.Copy))
                    psum.give(bank, m)
                    state["xT_ready"][g] = m
                    yield

        def route(layer, s, state):
            rows = state["rows"][s]
            while not psum.has(1):
                yield
            logits = psum.take()
            pe.need(*logits.freed, *(state["xT_ready"][s * gps + q] for q in range(gps)))
            for j in range(ST):
                m = pe_e.matmul(logits.ap[:, j * E:(j + 1) * E], xT[:, ST * s + j, :],
                                gates[:, layer * E:(layer + 1) * E], start=True, stop=True)
            m = pe.did(m)
            yield
            L = logits.ap[:, 0:ST * E].rearrange("p (a b) -> p a b", b=E)
            score, m1, m2, less, tmp, place, tmp2 = (r[:] for r in R8)

            def over_e(a):
                return a.unsqueeze(2).to_broadcast([P, ST, E])

            def over_j(a):
                return a.unsqueeze(1).to_broadcast([P, ST, E])

            best, second, z, p1, p2, den, w1, w2, e2, sl = (r[:] for r in R1)

            def v(ins):
                m = dve.did(ins)
                dve.need(m)
                return m

            dve.need(m)
            v(dve_e.tensor_reduce(best, L, AX, ALU.max))
            v(dve_e.tensor_tensor(tmp, L, over_e(best), ALU.is_equal))
            v(dve_e.tensor_tensor(tmp, tmp, over_j(const("first")), ALU.mult))
            v(dve_e.tensor_reduce(second, tmp, AX, ALU.max))
            yield
            v(dve_e.tensor_tensor(m1, tmp, over_e(second), ALU.is_equal))
            v(dve_e.scalar_tensor_tensor(less, m1, -BIG, L, ALU.mult, ALU.add))
            v(dve_e.tensor_reduce(second, less, AX, ALU.max))
            yield
            v(dve_e.tensor_tensor(tmp, less, over_e(second), ALU.is_equal))
            v(dve_e.tensor_tensor(tmp, tmp, over_j(const("first")), ALU.mult))
            v(dve_e.tensor_reduce(e2, tmp, AX, ALU.max))
            v(dve_e.tensor_tensor(m2, tmp, over_e(e2), ALU.is_equal))
            yield
            chosen = v(dve_e.tensor_tensor(choice_bf[:], m1, m2, ALU.add))
            shifted = v(dve_e.tensor_tensor(score, L, over_e(best), ALU.subtract))
            psum.give(logits, shifted)
            act.need(shifted)
            exps = act.did(act_e.activation(score, score, ACT.Exp))
            yield
            while not psum.has(1):
                yield
            ranks = psum.take()
            pe.need(chosen, *ranks.freed)
            flat = choice_bf[:].rearrange("p a b -> p (a b)")
            pe_e.matmul(ranks.ap[:, 0:ST * E], before_bf[:], flat, start=True, stop=True)
            m = pe.did(pe_e.matmul(ranks.ap[:, ST * E:2 * ST * E], ones_bf[:], flat, start=True, stop=True))
            yield
            dve.need(m)
            v(dve_e.tensor_copy(scan[0][:, 8:, :], ranks.ap[:, ST * E:2 * ST * E].rearrange("p (a b) -> p a b", b=E)))
            for i, d in enumerate((1, 2, 4, 8)):
                a, b = scan[i % 2], scan[(i + 1) % 2]
                v(dve_e.tensor_tensor(b[:, 8:, :], a[:, 8:, :], a[:, 8 - d:8 + ST - d, :], ALU.add))
                if i % 2:
                    yield
            v(dve_e.tensor_tensor(place, ranks.ap[:, 0:ST * E].rearrange("p (a b) -> p a b", b=E),
                                  scan[0][:, 7:7 + ST, :], ALU.add))
            psum.give(ranks, (dve.sem, dve.n))
            old = const("regions") if s == 0 else base[s % 2][:]
            v(dve_e.tensor_tensor(place, place, over_j(old), ALU.add))
            v(dve_e.tensor_tensor(base[(s + 1) % 2][:], old, scan[0][:, 7 + ST, :], ALU.add))
            for k, mk in enumerate((m1, m2)):
                v(dve_e.tensor_tensor(tmp, place, mk, ALU.mult))
                v(dve_e.tensor_reduce(sl, tmp, AX, ALU.add))
                placed = v(dve_e.tensor_copy(slot_i[k][:, s % 2, :], sl))
                yield
            dve.need(exps)
            v(dve_e.tensor_reduce(z, score, AX, ALU.add))
            v(dve_e.reciprocal(p1, z))
            v(dve_e.tensor_tensor(tmp2, score, m2, ALU.mult))
            v(dve_e.tensor_reduce(e2, tmp2, AX, ALU.add))
            yield
            v(dve_e.tensor_tensor(p2, e2, p1, ALU.mult))
            v(dve_e.scalar_tensor_tensor(den, p1, GATE_EPS if layer == 0 else 0.0, p2, ALU.add, ALU.add))
            v(dve_e.reciprocal(sl, den))
            dve.did(dve_e.tensor_tensor(rows.ap[:, :, 0, C + 1], p1, sl, ALU.mult))
            dve.did(dve_e.tensor_tensor(rows.ap[:, :, 1, C + 1], p2, sl, ALU.mult))
            for k in range(K):
                filled = dve.did(dve_e.tensor_copy(rows.ap[:, :, k, C].bitcast(I32),
                                                   addresses[:, k, ST * s:ST * s + ST]))
            state["routed"][s] = (placed, filled, state["copied"][s])

        def send(layer, s, state):
            rows = state["rows"][s]
            pool.need(*state["routed"][s])
            for j in range(ST):
                for k in range(K):
                    m = rows.arrival.by(pool_e.indirect_dma_start(
                        out=sent, out_offset=bass.IndirectOffsetOnAxis(ap=slot_i[k][:, s % 2, j:j + 1], axis=0),
                        in_=rows.ap[:, j, k, :], in_offset=None))
                yield
            state["sent"][s % 2] = m
            rings["rows"].give(rows, m)

        def plan(layer, state):
            last = base[NS % 2]
            scratch = rings["stage"].take()
            dve.need(*scratch.freed)
            table_8 = scratch.ap[0:1, 0:2 * NTILES * E].rearrange("p (a b c) -> p a b c", a=2, b=NTILES)
            table_f = scratch.ap[0:1, 2 * NTILES * E:(2 * E + 5) * NTILES].rearrange("p (a b) -> p a b", b=NTILES)

            def v(ins):
                m = dve.did(ins)
                dve.need(m)
                return m

            n, up, c0, c1, nt, _ = (counts_8[:, i, 8:] for i in range(6))
            v(dve_e.tensor_copy(starts_i[layer][:], last[0:1, :]))
            v(dve_e.tensor_tensor(n, last[0:1, :], const("regions")[0:1, :], ALU.subtract))
            v(dve_e.tensor_scalar(counts_i[:, 0, :], n, float(SLOTS - 1), None, ALU.add))
            v(dve_e.tensor_scalar(counts_i[:, 1, :], counts_i[:, 0, :], SLOTS.bit_length() - 1, None,
                                  ALU.logical_shift_right))
            v(dve_e.tensor_copy(nt, counts_i[:, 1, :]))
            v(dve_e.tensor_copy(c0, nt))
            for i, d in enumerate((1, 2, 4)):
                a, b = 2 + i % 2, 2 + (i + 1) % 2
                v(dve_e.tensor_tensor(counts_8[:, b, 8:], counts_8[:, a, 8:], counts_8[:, a, 8 - d:8 + E - d], ALU.add))
            ends = counts_8[:, 3, 8:]
            tiles = const("tiles")[0:1, :]
            past, mine = table_8[:, 0, :, :], table_8[:, 1, :, :]
            shape = [1, NTILES, E]
            v(dve_e.tensor_tensor(past, tiles.unsqueeze(2).to_broadcast(shape),
                                  ends.unsqueeze(1).to_broadcast(shape), ALU.is_ge))
            v(dve_e.tensor_tensor(mine, past, nt.unsqueeze(1).to_broadcast(shape), ALU.mult))
            f = [table_f[:, i, :] for i in range(5)]
            v(dve_e.tensor_reduce(f[0], past, AX, ALU.add))
            v(dve_e.tensor_reduce(f[1], mine, AX, ALU.add))
            v(dve_e.tensor_tensor(f[2], tiles, f[1], ALU.subtract))
            v(dve_e.tensor_scalar(f[3], f[0], float(REGION), None, ALU.mult))
            v(dve_e.scalar_tensor_tensor(f[4], f[2], float(SLOTS), f[3], ALU.mult, ALU.add))
            v(dve_e.tensor_copy(table_i[layer][:, 1, :], f[4]))
            m = v(dve_e.tensor_scalar(table_i[layer][:, 0, :], f[0], float(E - 1), None, ALU.min))
            rings["stage"].give(scratch, m)
            sp.need(m, pads_kept)
            for e in range(E):
                r = sp_e.value_load(starts_i[layer][0:1, e:e + 1], min_val=0, max_val=DUMMY - SLOTS)
                pad_arrival.by(sp_e.dma_start(sent[bass.ds(r, SLOTS), :].rearrange("(s p) c -> p s c", p=P),
                                              padding[e * SLOTS:(e + 1) * SLOTS, :].rearrange("(s p) c -> p s c", p=P)))
                yield

        def add_bias(o, a, b):
            pe_e.matmul(o, ones_r[:], brow_hi[:, a:b], start=False, stop=False)
            return pe_e.matmul(o, ones_r[:], brow_lo[:, a:b], start=False, stop=True)

        def attention0(g, state):
            xg = xT[:, GT * g:GT * g + GT, :]
            pe.need(state["xT_ready"][g], weights_here)
            while not psum.has(3):
                yield
            q_ps = psum.take()
            pe.need(*q_ps.freed)
            m_q = pe.did(pe_e.matmul(q_ps.ap[:], w_attn0[:, 0:C], xg.rearrange("p a b -> p (a b)"), start=True, stop=True))
            kv_ps, m_kv = [], []
            for h in range(2):
                bank = psum.take()
                pe.need(*bank.freed)
                for i in range(2):
                    o = bank.ap[:, 2 * C * i:2 * C * (i + 1)]
                    pe_e.matmul(o, xg[:, 2 * h + i, :], w_attn0[:, C:3 * C], start=True, stop=False)
                    m = add_bias(o, 0, 2 * C)
                kv_ps.append(bank)
                m_kv.append(pe.did(m))
            yield
            while not big.has(5):
                yield
            q, q_e = big.take(), big.take()
            act.need(m_q, *q_e.freed)
            m = act.did(act_e.activation(q_e.ap[:], q_ps.ap[:], ACT.Exp, bias=cols[:, 0:1]))
            dve.need(m)
            m = dve.did(dve_e.tensor_scalar(q_e.ap[:], q_e.ap[:], 1.0, None, ALU.min))
            dve.need(m, *q.freed)
            q_ready = dve.did(dve_e.scalar_tensor_tensor(q.ap[:], q_ps.ap[:], bq0p1[:], q_e.ap[:], ALU.add, ALU.max))
            psum.give(q_ps, q_ready)
            big.give(q_e, q_ready)
            k, k_e, v = big.take(), big.take(), big.take()
            k_ready, v_ready = [], []
            for h in range(2):
                src = kv_ps[h].ap[:].rearrange("p (a b) -> p a b", b=2 * C)
                c0, c1 = 2 * C * h, 2 * C * (h + 1)

                def half(s):
                    return s.ap[:, c0:c1].rearrange("p (a b) -> p a b", b=C)

                act.need(m_kv[h], *k_e.freed)
                m = act.did(act_e.activation(half(k_e), src[:, :, 0:C], ACT.Exp))
                act.need(*v.freed)
                v_ready.append(act.did(act_e.activation(half(v), src[:, :, C:2 * C], ACT.Copy)))
                dve.need(m)
                m = dve.did(dve_e.tensor_scalar(half(k_e), half(k_e), 1.0, None, ALU.min))
                dve.need(m, v_ready[h], *k.freed)
                k_ready.append(dve.did(dve_e.scalar_tensor_tensor(half(k), src[:, :, 0:C], 1.0, half(k_e), ALU.add, ALU.max)))
                psum.give(kv_ps[h], k_ready[h])
            big.give(k_e, *k_ready)
            yield from pause("kv0")
            while not psum.has(1):
                yield
            kv_bank = psum.take()
            pe.need(*kv_bank.freed)
            for h in range(2):
                pe.need(k_ready[h], v_ready[h])
                for i in range(2):
                    sl = slice((2 * h + i) * C, (2 * h + i + 1) * C)
                    m = pe_e.matmul(kv_bank.ap[:, h * P:(h + 1) * P], v.ap[:, sl], k.ap[:, sl], start=(i == 0), stop=(i == 1))
            m = pe.did(m)
            big.give(k, m)
            big.give(v, m)
            while not big.has(1):
                yield
            kvT = big.take()
            dve.need(m, *kvT.freed)
            m = dve.did(dve_e.tensor_tensor(kvT.ap[:, 0:2 * P].rearrange("p (a b) -> p a b", b=P),
                                            kv_bank.ap[:, 0:2 * P].rearrange("p (a b) -> p a b", b=P),
                                            const("heads0").unsqueeze(1).to_broadcast([P, 2, P]), ALU.mult))
            psum.give(kv_bank, m)
            yield from pause("mix0")
            while not psum.has(1):
                yield
            mix_bank = psum.take()
            pe.need(m, *mix_bank.freed)
            for h in range(2):
                m = pe_e.matmul(mix_bank.ap[:, h * C:(h + 1) * C], kvT.ap[:, h * P:(h + 1) * P], w_attn0[:, 3 * C:4 * C],
                                start=True, stop=True)
            m = pe.did(m)
            big.give(kvT, m)
            while not big.has(1):
                yield
            mix = big.take()
            act.need(m, *mix.freed)
            m = act.did(act_e.activation(mix.ap[:, 0:2 * C], mix_bank.ap[:, 0:2 * C], ACT.Copy))
            psum.give(mix_bank, m)
            yield from pause("y0")
            while not psum.has(1):
                yield
            y = psum.take()
            pe.need(q_ready, m, *y.freed)
            for i in range(GT):
                o = y.ap[:, i * C:(i + 1) * C]
                pe_e.matmul(o, q.ap[:, i * P:(i + 1) * P], mix.ap[:, (i // 2) * C:(i // 2 + 1) * C], start=True, stop=False)
                m = add_bias(o, 2 * C, 3 * C)
            m = pe.did(m)
            big.give(q, m)
            big.give(mix, m)
            xr = X[:, GT * g:GT * g + GT, :].rearrange("p a b -> p (a b)")
            dve.need(m, state["rows_read"][g])
            m = dve.did(dve_e.tensor_tensor(xr, xr, y.ap[:], ALU.add))
            psum.give(y, m)
            state["X_after"][g] = m

        def shared(g, state):
            xg = xT[:, GT * g:GT * g + GT, :].rearrange("p a b -> p (a b)")
            pe.need(state["xT_ready"][g], weights_here)
            h = []
            for c0, n in FSC:
                while not (psum.has(2) and big.has(2)):
                    yield
                gate, up = psum.take(), psum.take()
                pe.need(*gate.freed)
                m_g = pe.did(pe_e.matmul(gate.ap[0:n, :], w_shared[:, c0:c0 + n], xg, start=True, stop=True))
                pe.need(*up.freed)
                m_u = pe.did(pe_e.matmul(up.ap[0:n, :], w_shared[:, FS + c0:FS + c0 + n], xg, start=True, stop=True))
                s, hc = big.take(), big.take()
                act.need(m_g, *s.freed)
                m = act.did(act_e.activation(s.ap[0:n, :], gate.ap[0:n, :], ACT.Tanh, scale=0.5))
                yield
                dve.need(m)
                m = dve.did(dve_e.scalar_tensor_tensor(s.ap[0:n, :], s.ap[0:n, :], 1.0, gate.ap[0:n, :], ALU.add, ALU.mult))
                psum.give(gate, m)
                dve.need(m, m_u, *hc.freed)
                m = dve.did(dve_e.tensor_tensor(hc.ap[0:n, :], s.ap[0:n, :], up.ap[0:n, :], ALU.mult))
                psum.give(up, m)
                big.give(s, m)
                h.append((hc, m, n))
                yield
            state["xT_free"][g] = (m_u,)
            yield from pause("down")
            while not (psum.has(1) and "made" in weights):
                yield
            y = psum.take()
            pe.need(weights["made"], *y.freed, *(m for _, m, _ in h))
            for i in range(GT):
                for c, (hc, _, n) in enumerate(h):
                    m = pe_e.matmul(y.ap[:, i * C:(i + 1) * C], hc.ap[0:n, i * P:(i + 1) * P],
                                    w_shared[0:n, 2 * FS + c * C:2 * FS + (c + 1) * C], start=(c == 0), stop=(c == 2))
            m = pe.did(m)
            for hc, _, _ in h:
                big.give(hc, m)
            xr = X[:, GT * g:GT * g + GT, :].rearrange("p a b -> p (a b)")
            while g not in state["X_after"]:
                yield
            dve.need(m, state["X_after"][g])
            m = dve.did(dve_e.tensor_tensor(xr, xr, y.ap[:], ALU.add))
            psum.give(y, m)
            state["X_last"][g] = m

        return_marks = {}

        def fetch(layer, n, state):
            while not (rings["stage"].has(1) and rings["tile_in"].has(1)):
                yield
            w, r = rings["stage"].take(), rings["tile_in"].take()
            if n == 0:
                sp.need(*state["sent"], pad_arrival.all)
            ncols = (W0COLS, W1COLS)[layer]
            e = sp_e.value_load(table_i[layer][0:1, 0, n:n + 1], min_val=0, max_val=E - 1)
            first = sp_e.value_load(table_i[layer][0:1, 1, n:n + 1], min_val=0, max_val=DUMMY + (NDUMMY - 1) * SLOTS)
            sp.need(*r.freed)
            r_here = r.arrival.by(sp_e.dma_start(
                r.ap[:], sent[bass.ds(first, SLOTS), :].rearrange("(s p) c -> p s c", p=P)))
            sp.need(*w.freed)
            w_here = w.arrival.by(sp_e.dma_start(
                w.ap[:, 0:ncols], t[f"experts{layer}"][bass.ds(e, 1), :, :].rearrange("a p n -> p (a n)")))
            state["fetched"][n] = (w, r, w_here, r_here)

        def split(hi, lo, src, ready):
            hi_r, lo_r = (s.ap[:, 0:src.shape[1]] for s in (hi, lo))
            act.need(ready, *hi.freed)
            m = act.did(act_e.activation(hi_r, src, ACT.Copy))
            dve.need(m, ready, *lo.freed)
            return dve.did(dve_e.tensor_tensor(lo_r, src, hi_r.bitcast(F32), ALU.subtract))

        def product(out, w_hi, w_lo, c0, x_hi, x_lo):
            wh, wl = w_hi.ap[:, c0:c0 + P], w_lo.ap[:, c0:c0 + P]
            xh, xl = x_hi.ap[:, 0:SLOTS], x_lo.ap[:, 0:SLOTS]
            pe_e.matmul(out, wh, xh, start=True, stop=False)
            pe_e.matmul(out, wh, xl, start=False, stop=False)
            return pe_e.matmul(out, wl, xh, start=False, stop=True)

        def expert_tile(layer, n, state):
            w, r, w_here, r_here = state["fetched"][n]
            up_cols = (2 * F0P, F1)[layer]
            while not rings["parts"].has(4):
                yield
            w_hi, w_lo, x_hi, x_lo = (rings["parts"].take() for _ in range(4))
            m_w = split(w_hi, w_lo, w.ap[:, 0:up_cols], w_here)
            while not psum.has(1):
                yield
            bank = psum.take()
            pe.need(r_here, *bank.freed)
            for i in range(SUB):
                m = pe_e.transpose(bank.ap[:, i * P:(i + 1) * P], r.ap[:, i, 0:C], ident)
            m = pe.did(m)
            x_ready = split(x_hi, x_lo, bank.ap[:], m)
            psum.give(bank, x_ready)
            yield
            yield
            yield
            pe.need(w_here, m_w, x_ready)
            h = []
            if layer == 0:
                while not (psum.has(3) and big.has(4)):
                    yield
                gate, up, tail = psum.take(), psum.take(), psum.take()
                pe.need(*gate.freed)
                m_g = pe.did(product(gate.ap[:], w_hi, w_lo, 0, x_hi, x_lo))
                pe.need(*up.freed)
                m_u = pe.did(product(up.ap[:], w_hi, w_lo, F0P + 64, x_hi, x_lo))
                pe.need(*tail.freed)
                m_t = pe.did(product(tail.ap[:], w_hi, w_lo, P, x_hi, x_lo))
                for slot in (w_hi, w_lo, x_hi, x_lo):
                    rings["parts"].give(slot, m_t)
                for n_h, src_g, src_u, m1, m2, slots in ((P, gate.ap, up.ap, m_g, m_u, (gate, up)),
                                                         (F0T, tail.ap, tail.ap[64:64 + F0T, :], m_t, m_t, (tail,))):
                    s, hc = big.take(), big.take()
                    act.need(m1, *s.freed)
                    m = act.did(act_e.activation(s.ap[0:n_h, :], src_g[0:n_h, :], ACT.Silu))
                    dve.need(m, m2, *hc.freed)
                    m = dve.did(dve_e.tensor_tensor(hc.ap[0:n_h, :], s.ap[0:n_h, :], src_u[0:n_h, :], ALU.mult))
                    for slot in slots:
                        psum.give(slot, m)
                    big.give(s, m)
                    h.append((hc, m, n_h))
                down, b1, b2 = 2 * F0P, None, None
            else:
                b1 = F1 + NC1 * C
                b2 = b1 + NC1
                down = F1
                for c in range(NC1):
                    while not (psum.has(1) and big.has(1)):
                        yield
                    z = psum.take()
                    pe.need(*z.freed)
                    m = pe.did(product(z.ap[:], w_hi, w_lo, c * P, x_hi, x_lo))
                    hc = big.take()
                    act.need(m, w_here, *hc.freed)
                    m1 = act.did(act_e.activation(hc.ap[:], z.ap[:], ACT.Gelu, bias=w.ap[:, b1 + c:b1 + c + 1]))
                    psum.give(z, m1)
                    h.append((hc, m1, P))
                    if c % 2 == 1 and c < NC1 - 1:
                        yield
                for slot in (w_hi, w_lo, x_hi, x_lo):
                    rings["parts"].give(slot, m)
            yield
            yield
            while not (psum.has(1) and rings["tile_out"].has(1)):
                yield
            y = psum.take()
            pe.need(*y.freed, *(m for _, m, _ in h))
            for i in range(SUB):
                for c, (hc, _, k) in enumerate(h):
                    m = pe_e.matmul(y.ap[:, i * C:(i + 1) * C], hc.ap[0:k, i * P:(i + 1) * P],
                                    w.ap[0:k, down + c * C:down + (c + 1) * C], start=(c == 0), stop=(c == len(h) - 1))
            m_y = pe.did(m)
            for hc, _, _ in h:
                big.give(hc, m_y)
            o = rings["tile_out"].take()
            src = y.ap[:].rearrange("p (a b) -> p a b", b=C)
            dve.need(m_y, r_here, *o.freed)
            if layer == 1:
                dve.need(w_here)
                m = dve.did(dve_e.tensor_tensor(o.ap[:], src, w.ap[:, b2:b2 + C].unsqueeze(1).to_broadcast([P, SUB, C]), ALU.add))
                dve.need(m)
                psum.give(y, m)
                src = o.ap[:]
            m = dve.did(dve_e.tensor_tensor(o.ap[:], src, r.ap[:, :, C + 1:C + 2].to_broadcast([P, SUB, C]), ALU.mult))
            if layer == 0:
                psum.give(y, m)
            rings["stage"].give(w, m_y, m)
            yield
            pool.need(m)
            for i in range(SUB):
                m = o.arrival.by(pool_e.indirect_dma_start(
                    out=back, out_offset=bass.IndirectOffsetOnAxis(ap=r.ap[:, i, C:C + 1].bitcast(I32), axis=0),
                    in_=o.ap[:, i, :], in_offset=None))
            rings["tile_out"].give(o, m)
            rings["tile_in"].give(r, m)
            return_marks[o.arrival.sem.name] = m

        def collect(g, state):
            while not joined.has(K):
                yield
            sp.need(*return_marks.values())
            parts = []
            for k in range(K):
                part = joined.take()
                sp.need(*part.freed)
                rows = slice(k * TOK + g * GT * P, k * TOK + (g + 1) * GT * P)
                parts.append((part, part.arrival.by(sp_e.dma_start(
                    part.ap[:], back[rows, :].rearrange("(s p) c -> p s c", p=P)))))
            yield
            xr = X[:, GT * g:GT * g + GT, :]
            for part, here in parts:
                while g not in state["X_before"]:
                    yield
                dve.need(here, state["X_before"][g])
                m = dve.did(dve_e.tensor_tensor(xr, xr, part.ap[:], ALU.add))
                joined.give(part, m)
                state["X_before"][g] = m
            state["X_done"][g] = m

        joined = ring("joined", 4, [P, GT, C], dma=True)

        def attention1(g, state):
            xg = xT[:, GT * g:GT * g + GT, :]
            flat = xg.rearrange("p a b -> p (a b)")
            ready = []
            while not (big.has(HEADS64 + 5) and v_heads.has(1) and psum.has(4)):
                yield
            q, k, kh = big.take(), big.take(), [big.take() for _ in range(HEADS64)]
            v = v_heads.take()
            pe.need(state["xT_ready"][g])
            for c, dst in ((0, q), (1, k)):
                bank, e = psum.take(), big.take()
                pe.need(*bank.freed)
                m = pe.did(pe_e.matmul(bank.ap[:], w_attn1[:, c * C:(c + 1) * C], flat, start=True, stop=True))
                act.need(m, *e.freed)
                m = act.did(act_e.activation(e.ap[:], bank.ap[:], ACT.Exp, bias=cols[:, 1 + c:2 + c]))
                dve.need(m)
                m = dve.did(dve_e.tensor_scalar(e.ap[:], e.ap[:], 1.0, -1.0, ALU.min, ALU.add))
                dve.need(m, *dst.freed)
                m = dve.did(dve_e.scalar_tensor_tensor(dst.ap[:], bank.ap[:], cols[:, 1 + c:2 + c], e.ap[:], ALU.add, ALU.max))
                psum.give(bank, m)
                big.give(e, m)
                ready.append(m)
                yield from pause("qk1")
            q_ready, k_ready = ready
            while not (psum.has(1) and big.has(1)):
                yield
            bank, th = psum.take(), big.take()
            pe.need(*bank.freed)
            for i in range(GT):
                o = bank.ap[:, C * i:C * (i + 1)]
                pe_e.matmul(o, xg[:, i, :], w_attn1[:, 2 * C:3 * C], start=True, stop=False)
                m = add_bias(o, 3 * C, 4 * C)
            m = pe.did(m)
            act.need(m, *th.freed)
            m = act.did(act_e.activation(th.ap[:], bank.ap[:], ACT.Tanh, scale=0.5))
            dve.need(m, *v.freed)
            for s in range(HEADS32):
                dst, t_s, z_s = (a.rearrange("p (n s d) -> p n s d", s=HEADS32, d=D1)[:, :, s, :]
                                 for a in (v.ap[:, s, :, :].rearrange("p i c -> p (i c)"), th.ap[:], bank.ap[:]))
                m = dve.did(dve_e.scalar_tensor_tensor(dst, t_s, 1.0, z_s, ALU.add, ALU.mult))
            psum.give(bank, m)
            big.give(th, m)
            v_ready = m
            kh_ready = []
            for s in range(HEADS64):
                own = const("head_of_64")[:, s:s + 1]
                act.need(k_ready, *kh[s].freed)
                kh_ready.append(act.did(act_e.activation(kh[s].ap[:], k.ap[:], ACT.Copy, scale=own)))
            yield
            while not (psum.has(1) and big.has(2)):
                yield
            bank, th, u = psum.take(), big.take(), big.take()
            pe.need(*bank.freed)
            m = pe.did(pe_e.matmul(bank.ap[:], w_attn1[:, 3 * C:4 * C], flat, start=True, stop=True))
            act.need(m, *th.freed, *u.freed)
            act.did(act_e.activation(th.ap[:], bank.ap[:], ACT.Tanh, bias=half_bu[:], scale=0.5))
            m = act.did(act_e.activation(u.ap[:], bank.ap[:], ACT.Identity, bias=cols[:, 4:5]))
            psum.give(bank, m)
            dve.need(m)
            u_ready = dve.did(dve_e.scalar_tensor_tensor(u.ap[:], th.ap[:], 1.0, u.ap[:], ALU.add, ALU.mult))
            big.give(th, u_ready)
            yield
            while not (psum.has(1) and small2.has(1)):
                yield
            bank = psum.take()
            pe.need(k_ready, *bank.freed)
            for h in range(2):
                m = pe_e.transpose(bank.ap[:, h * P:(h + 1) * P], k.ap[:, 2 * h * P:(2 * h + 1) * P], ident)
            m = pe.did(m)
            k_tok = small2.take()
            act.need(m, *k_tok.freed)
            k_tok_ready = act.did(act_e.activation(k_tok.ap[:], bank.ap[:, 0:2 * P], ACT.Copy))
            psum.give(bank, k_tok_ready)
            big.give(k, m)
            yield
            while not (psum.has(1) and small2.has(1)):
                yield
            kv_bank = psum.take()
            pe.need(k_tok_ready, v_ready, *kv_bank.freed)
            for h in range(2):
                for s in range(HEADS32):
                    m = pe_e.matmul(kv_bank.ap[:, h * P:(h + 1) * P], k_tok.ap[:, h * P:(h + 1) * P], v.ap[:, s, 2 * h, :],
                                    start=(s == 0), stop=(s == HEADS32 - 1))
            m = pe.did(m)
            small2.give(k_tok, m)
            kv = small2.take()
            dve.need(m, *kv.freed)
            kv_ready = dve.did(dve_e.tensor_tensor(kv.ap[:].rearrange("p (a b) -> p a b", b=P),
                                                   kv_bank.ap[:, 0:2 * P].rearrange("p (a b) -> p a b", b=P),
                                                   const("heads1").unsqueeze(1).to_broadcast([P, 2, P]), ALU.mult))
            psum.give(kv_bank, kv_ready)
            yield
            while not (psum.has(3) and big.has(2)):
                yield
            att_bank = psum.take()

            def energies(h, j):
                bank, energy = psum.take(), big.take()
                rows64 = slice(64 * (j // 2), 64 * (j // 2) + 64)
                pe.need(q_ready, *kh_ready, *bank.freed)
                for i in range(2):
                    for s in range(HEADS32):
                        tok = slice((2 * h + i) * P, (2 * h + i + 1) * P)
                        m = pe_e.matmul(bank.ap[:, (2 * i + s) * P:(2 * i + s + 1) * P],
                                        kh[HEADS32 * (j % 2) + s].ap[rows64, tok], q.ap[rows64, tok],
                                        start=True, stop=True)
                m = pe.did(m)
                if j % 2:
                    dve.need(m, *energy.freed)
                    m = dve.did(dve_e.tensor_tensor(energy.ap[:].rearrange("p (a b) -> p a b", b=P),
                                                    bank.ap[:].rearrange("p (a b) -> p a b", b=P),
                                                    const("causal").unsqueeze(1).to_broadcast([P, 4, P]), ALU.mult))
                    psum.give(bank, m)
                else:
                    act.need(m, *energy.freed)
                    m = act.did(act_e.activation(energy.ap[:], bank.ap[:], ACT.Copy, scale=0.5))
                    psum.give(bank, m)
                    pool.need(m)
                    blocks = energy.ap[:].rearrange("p (a b) -> p a b", b=P)
                    m = pool.did(pool_e.affine_select(out=blocks, in_=blocks, pattern=[[0, 4], [1, P]], compare_op=ALU.is_ge,
                                                      fill=0.0, base=0, channel_multiplier=-1))
                return energy, m

            def gather(h, j, energy, masked):
                pe.need(masked)
                for i in range(2):
                    for s in range(HEADS32):
                        tile = 2 * h + i
                        m = pe_e.matmul(att_bank.ap[32 * j:32 * j + 32, tile * P:(tile + 1) * P],
                                        v.ap[:, s, tile, 32 * j:32 * j + 32], energy.ap[:, (2 * i + s) * P:(2 * i + s + 1) * P],
                                        start=False, stop=(h == 1 and i == 1 and s == HEADS32 - 1), skip_group_check=True)
                m = pe.did(m)
                big.give(energy, m)
                return m

            pending = []
            for h in range(2):
                for j in range(H1 // HEADS32):
                    while not (psum.has(1) and big.has(1)):
                        yield
                    pending.append((h, j, *energies(h, j)))
                    if h == 0 and j == 0:
                        pe.need(kv_ready, *att_bank.freed)
                        for b in range(2):
                            tile = 2 * b + 1
                            m = pe_e.matmul(att_bank.ap[:, tile * P:(tile + 1) * P], kv.ap[:, b * P:(b + 1) * P],
                                            q.ap[:, tile * P:(tile + 1) * P], start=(b == 0), stop=False, skip_group_check=True)
                        small2.give(kv, pe.did(m))
                    yield
                    if len(pending) > PENDING:
                        m = gather(*pending.pop(0))
            while pending:
                m = gather(*pending.pop(0))
            att_done = m
            big.give(q, m)
            for s in kh:
                big.give(s, m)
            v_heads.give(v, m)
            while not (big.has(2) and sums.has(1) and psum.has(1)):
                yield
            sq, uo, ss, bank = big.take(), big.take(), sums.take(), psum.take()
            dve.need(att_done, u_ready, *uo.freed)
            uo_ready = dve.did(dve_e.tensor_tensor(uo.ap[:], att_bank.ap[:], u.ap[:], ALU.mult))
            act.need(uo_ready, *sq.freed)
            m_sq = act.did(act_e.activation(sq.ap[:], att_bank.ap[:], ACT.Square))
            psum.give(att_bank, uo_ready, m_sq)
            big.give(u, uo_ready)
            yield from pause("squares")
            xr = X[:, GT * g:GT * g + GT, :]
            pool.need(state["X_done"][g], state["rows_read"][g])
            biased = pool.did(pool_e.tensor_tensor(xr, xr, bo1[:].unsqueeze(1).to_broadcast([P, GT, C]), ALU.add))
            pe.need(m_sq, *bank.freed)
            for i in range(GT):
                m = pe_e.matmul(bank.ap[:, i:i + 1], sq.ap[:, i * P:(i + 1) * P], ones[:], start=True, stop=True)
            m = pe.did(m)
            big.give(sq, m)
            tot = ss.ap[:, 3, :]
            dve.need(m, *ss.freed)
            m = dve.did(dve_e.tensor_copy(tot, bank.ap[:, 0:GT]))
            psum.give(bank, m)
            m = power(ss.ap[:, 0, :], tot, 0.5, (m, *ss.freed))
            yield from pause("root")
            dve.need(m)
            m = dve.did(dve_e.tensor_scalar(ss.ap[:, 1, :], ss.ap[:, 0, :], float(C) ** -0.5, RMS_EPS, ALU.mult, ALU.add))
            dve.need(m)
            inv_ready = dve.did(dve_e.reciprocal(ss.ap[:, 5, :], ss.ap[:, 1, :]))
            yield
            while not psum.has(1):
                yield
            y = psum.take()
            pe.need(uo_ready, weights["made"], *y.freed)
            for i in range(GT):
                m = pe_e.matmul(y.ap[:, i * C:(i + 1) * C], uo.ap[:, i * P:(i + 1) * P], wo1s, start=True, stop=True)
            m_y = pe.did(m)
            big.give(uo, m_y)
            dve.need(m_y, inv_ready, biased)
            for i in range(GT):
                m = dve.did(dve_e.scalar_tensor_tensor(X[:, GT * g + i, :], y.ap[:, i * C:(i + 1) * C], ss.ap[:, 5, i:i + 1],
                                                       X[:, GT * g + i, :], ALU.mult, ALU.add))
            psum.give(y, m)
            sums.give(ss, m)
            state["X_after"][g] = m

        small2 = ring("small2", 5, [P, 2 * P])
        sums = ring("sums", 3, [P, 6, GT])

        def use_buffers(**wanted):
            last = {}
            if scopes:
                for slot in scope_slots:
                    for s, n in slot.freed:
                        last[s.name] = max(last.get(s.name, (s, 0)), (s, n), key=lambda mark: mark[1])
                for slot in scope_slots:
                    if slot in big.free:
                        big.free.remove(slot)
                scopes[-1].close()
            scope_slots.clear()
            scope = ExitStack()
            scopes.append(scope)
            for name, (n, shape, dt, dma) in wanted.items():
                rings[name] = ring(name, n, shape, dt, dma, scope)
                for slot in rings[name].free:
                    slot.freed = tuple(last.values())
                    scope_slots.append(slot)
            if "more" in wanted:
                big.free.extend(rings["more"].free)

        scope_slots = []
        attention_buffers = {"rows": (2, [P, ST, K, ROW], F32, True), "more": (13, [P, 512], F32, False)}
        expert_buffers = {"stage": (5, [P, max(W0COLS, W1COLS)], F32, True), "tile_in": (7, [P, SUB, ROW], F32, True),
                          "tile_out": (3, [P, SUB, C], F32, True), "parts": (8, [P, SLOTS], F32R, False)}

        def new_state(**kw):
            return {"rows": {}, "rows_read": {}, "copied": {}, "routed": {}, "xT_ready": {}, "xT_free": {}, "X_done": {},
                    "X_after": {}, "X_last": {}, "sent": [None, None], "fetched": {}} | kw

        def when(d, *keys):
            return lambda: all(x in d for x in keys)

        def when_routed(layer, L, g):
            s = min(NS - 1, (g + AHEAD[layer]) // gps - 1)
            return lambda: g in L["xT_ready"] and (s < 0 or s in L["routed"])

        def always():
            return True

        wo1s = w_attn1[:, 4 * C:5 * C]
        weights = {}

        def prepare_weights():
            yield
            yield
            dve.need(weights_here)
            dve.did(dve_e.tensor_scalar(wo1s, wo1s, cols[:, 3:4], 0.5, ALU.mult, ALU.mult))
            weights["made"] = dve.did(dve_e.tensor_scalar(w_shared[:, 2 * FS:], w_shared[:, 2 * FS:], 0.5, None, ALU.mult))
            half_bu_made = dve.did(dve_e.tensor_scalar(half_bu[:], cols[:, 4:5], 0.5, None, ALU.mult))
            act.need(half_bu_made)

        def lanes_of(layer, L, attention, depth_gap):
            lanes = [
                Lane([(when_routed(layer, L, g), attention(g, L)) for g in range(NG)], *depth_gap),
                Lane([(always, normalise(layer, s, L)) for s in range(NS)], 1),
                Lane([(when(L["xT_ready"], *range(s * gps, (s + 1) * gps)), route(layer, s, L)) for s in range(NS)], 1),
                Lane([(when(L["routed"], s), send(layer, s, L)) for s in range(NS)], 1),
            ]
            return [lanes[i] for i in ORDER[layer]]

        def fetches(layer, L):
            return Lane([(always, fetch(layer, n, L)) for n in range(NTILES)], 1)

        def experts(layer, L, gap):
            return Lane([(when(L["fetched"], n), expert_tile(layer, n, L)) for n in range(NTILES)], 4, gap, young_first=True)

        L0 = new_state(X_done={g: x_here[g].all for g in range(NG)})
        use_buffers(**attention_buffers)
        emit(*lanes_of(0, L0, attention0, ATT0),
             Lane([(always, prepare_weights())], 1),
             Lane([(when(L0["xT_ready"], g), shared(g, L0)) for g in range(NG - LATE - EARLY)], *SHARED))
        use_buffers(**expert_buffers)
        planned = Lane([(always, plan(0, L0))], 1)
        early_shared = Lane([(always, shared(g, L0)) for g in range(NG - LATE - EARLY, NG - LATE)], 2, 3)
        emit(planned, early_shared, fetches_0 := fetches(0, L0), until=early_shared)
        emit(planned, fetches_0, experts(0, L0, 2))

        use_buffers(**attention_buffers)
        L1 = new_state(xT_free=L0["xT_free"], X_before=L0["X_last"])
        emit(Lane([(always, shared(g, L0)) for g in range(NG - LATE, NG)], 1),
             Lane([(always, collect(g, L1)) for g in range(NG)], *COLLECT),
             *lanes_of(1, L1, attention1, ATT1))
        use_buffers(**expert_buffers)
        emit(Lane([(always, plan(1, L1))], 1), fetches(1, L1), experts(1, L1, 3))

        out_arrival = Arrival(sem("out_dma"))
        y_out = out.rearrange("(n p) c -> p n c", p=P)
        L2 = new_state(X_before=L1["X_after"])

        def finish(g, state):
            yield from collect(g, state)
            act.need(state["X_done"][g])
            out_arrival.by(act_e.dma_start(y_out[:, GT * g:GT * g + GT, :], X[:, GT * g:GT * g + GT, :]))

        emit(Lane([(always, finish(g, L2)) for g in range(NG)], 2))
        act.need(out_arrival.all)
        scopes[-1].close()


def kernel(**inputs):
    import concourse.bacc as bacc
    from concourse.bass_utils import run_bass_kernel_spmd

    i = {k: np.asarray(v) for k, v in inputs.items()}

    def padded(a, n):
        return np.concatenate([a, np.zeros((*a.shape[:-1], n - a.shape[-1]), a.dtype)], axis=-1)

    def padded_rows(a, n):
        return np.concatenate([a, np.zeros((*a.shape[:-2], n - a.shape[-2], a.shape[-1]), a.dtype)], axis=-2)

    wd = padded_rows(i["L0_ffn_wd"], 2 * P)
    wu = i["L0_ffn_wu"]
    experts0 = np.concatenate([padded(i["L0_ffn_wg"], F0P), padded(wu[:, :, P:], 64), wu[:, :, 0:P], wd[:, 0:P], wd[:, P:2 * P]], axis=2)
    w2 = i["L1_ffn_w2"].reshape(E, NC1, P, C).transpose(0, 2, 1, 3).reshape(E, P, NC1 * C)
    b1 = i["L1_ffn_b1"].reshape(E, NC1, P).transpose(0, 2, 1)
    b2 = np.broadcast_to(i["L1_ffn_b2"][:, None, :], (E, P, C))
    experts1 = np.concatenate([i["L1_ffn_w1"], w2, b1, b2], axis=2)
    swd = padded_rows(i["L0_ffn_swd"], 3 * P)
    arrays = {
        "x": i["L0_attn_x"].reshape(TOK, C),
        "consts": constants()[0],
        "addresses": return_addresses(),
        "pad_addresses": padding_addresses(),
        "gates": np.concatenate([i["L0_ffn_gate_w"].T, i["L1_ffn_w_router"].T], axis=1),
        "cols": np.stack([i["L0_attn_bq"], i["L1_attn_bq"], i["L1_attn_bk"], i["L1_attn_scale"], i["L1_attn_bu"]], axis=1),
        "brow": np.concatenate([i["L0_attn_bk"], i["L0_attn_bv"], i["L0_attn_bo"], i["L1_attn_bv"]])[None, :],
        "w_attn0": np.concatenate([i[f"L0_attn_W{n}"].T for n in "qkvo"], axis=1),
        "w_attn1": np.concatenate([i[f"L1_attn_W{n}"].T for n in "qkvuo"], axis=1),
        "w_shared": np.concatenate([i["L0_ffn_swg"], i["L0_ffn_swu"], swd[0:P], swd[P:2 * P], swd[2 * P:3 * P]], axis=1),
        "bo1": np.broadcast_to(i["L1_attn_bo"][None, :], (P, C)),
        "experts0": experts0,
        "experts1": experts1,
    }
    nc = bacc.Bacc("TRN2", target_bir_lowering=False, num_devices=1)
    feed, t = {}, {}
    for name, a in arrays.items():
        a = np.ascontiguousarray(a)
        feed[f"in_{name}"] = a
        t[name] = nc.dram_tensor(f"in_{name}", a.shape, mybir.dt.from_np(a.dtype), kind="ExternalInput").ap()
    out = nc.dram_tensor("out", (TOK, C), F32, kind="ExternalOutput").ap()
    build(nc, t, out)
    r = run_bass_kernel_spmd(nc, [feed], core_ids=[0])
    return r.results[0]["out"].reshape(B, S, C)
```
